# Optimizing a Trainium2 kernel written in Bass

```python
import numpy as np
import jax
import jax.numpy as jnp

def _softmax(x, axis=-1):
    return jax.nn.softmax(x, axis=axis)
def _gelu(x):
    return jax.nn.gelu(x, approximate=True)
def _silu(x):
    return jax.nn.silu(x)
def _sigmoid(x):
    return jax.nn.sigmoid(x)
def _layernorm(x, axis=-1, eps=1e-5):
    m = jnp.mean(x, axis=axis, keepdims=True)
    v = jnp.var(x, axis=axis, keepdims=True)
    return (x - m) / jnp.sqrt(v + eps)
def _scatter_add(tgt, idx, src, axis=0):
    return tgt.at[idx].add(src)
def _segment_sum(src, seg, n):
    return jax.ops.segment_sum(src, seg, n)

kernel_name = 'mk_adj_preln_d2_adj_128_ff5d53'

def setup_inputs(seed: int = 0):
    np.random.seed(seed)
    _w = jnp.asarray
    def _rec_inputs():
        import jax
        import jax.numpy as jnp
        _gk = jax.random.key(seed)
        x = -0.000929 + 1 * jax.random.normal(jax.random.fold_in(_gk, 1), (8192, 128), jnp.float32)
        _a = jax.random.bernoulli(jax.random.fold_in(_gk, 2), 0.000488281, (8192, 8192))
        adj = _a.astype(jnp.int32)
        return x, adj
    x, adj = _rec_inputs()
    def _L0_gnn_setup():
        import jax, jax.numpy as jnp
        import numpy as np
        NEG_BIG = -9000000000000000.0
        LEAKY_SLOPE = 0.2
        key = jax.random.key(seed)
        k1, k2, k3 = jax.random.split(key, 3)
        N, M, D = (8192, 8192, 128)
        qs = jax.random.normal(k1, (N, D), dtype=jnp.float32)
        ks = jax.random.normal(k2, (M, D), dtype=jnp.float32)
        HpGraph_e_k = jax.random.randint(k3, (N, M), 0, 2, dtype=jnp.int32)
        return {'qs': qs, 'ks': ks, 'HpGraph_e_k': HpGraph_e_k}
    _L0_gnn_all = _L0_gnn_setup()
    _L0_gnn_in = {k: v for k, v in _L0_gnn_all.items() if k in ('ks', )}
    del _L0_gnn_all

    def _L1_gnn_setup():
        import jax, jax.numpy as jnp
        import numpy as np
        N = 8192
        D_IN = 128
        D_OUT = 128
        ALPHA = 0.2
        NEG = -9000000000000000.0
        key = jax.random.key(seed)
        k1, k2, k3, k4 = jax.random.split(key, 4)
        input = jax.random.normal(k1, (N, D_IN), dtype=jnp.float32)
        adj = jax.random.randint(k2, (N, N), 0, 2, dtype=jnp.int32)
        lim_w = 1.414 * np.sqrt(6.0 / (D_IN + D_OUT))
        W = jax.random.uniform(k3, (D_IN, D_OUT), jnp.float32, -lim_w, lim_w)
        lim_a = 1.414 * np.sqrt(6.0 / (2 * D_OUT + 1))
        a = jax.random.uniform(k4, (2 * D_OUT, 1), jnp.float32, -lim_a, lim_a)
        return {'input': input, 'adj': adj, 'W': W, 'a': a}
    _L1_gnn_all = _L1_gnn_setup()
    _L1_gnn_in = {k: v for k, v in _L1_gnn_all.items() if k in ('W', 'a', )}
    del _L1_gnn_all

    return {
        "x": x,
        "adj": adj,
        "L0_gnn_ks": _L0_gnn_in["ks"],
        "L1_gnn_W": _L1_gnn_in["W"],
        "L1_gnn_a": _L1_gnn_in["a"],
    }

def reference(x, adj, L0_gnn_ks, L1_gnn_W, L1_gnn_a):
    import jax
    import jax.numpy as jnp
    def _L0_gnn_ref(qs, ks, HpGraph_e_k):
        import jax, jax.numpy as jnp
        import numpy as np
        NEG_BIG = -9000000000000000.0
        LEAKY_SLOPE = 0.2
        scores = jnp.einsum('nd,md->nm', qs, ks)
        scores = jax.nn.leaky_relu(scores, negative_slope=LEAKY_SLOPE)
        scores = jnp.where(HpGraph_e_k > 0, scores, NEG_BIG)
        attn = jax.nn.softmax(scores, axis=1)
        return jnp.einsum('nm,md->nd', attn, ks)

    def _L1_gnn_ref(input, adj, W, a):
        import jax, jax.numpy as jnp
        import numpy as np
        N = 8192
        D_IN = 128
        D_OUT = 128
        ALPHA = 0.2
        NEG = -9000000000000000.0
        h = input @ W
        a1 = a[:D_OUT, 0]
        a2 = a[D_OUT:, 0]
        e = (h @ a1)[:, None] + (h @ a2)[None, :]
        e = jnp.where(e > 0, e, ALPHA * e)
        e = jnp.where(adj > 0, e, NEG)
        attention = jax.nn.softmax(e, axis=1)
        h_prime = attention @ h
        return jax.nn.elu(h_prime)

    h = jnp.maximum(_layernorm(x, axis=-1), 0.0)
    x = x + _L0_gnn_ref(h, L0_gnn_ks, adj)
    h = jnp.maximum(_layernorm(x, axis=-1), 0.0)
    x = x + _L1_gnn_ref(h, adj, L1_gnn_W, L1_gnn_a)
    return x


_drawn_inputs = setup_inputs


def setup_inputs(seed=0):
    import zlib

    import numpy as np

    out = dict(_drawn_inputs(seed))
    spreads = {}
    factors = {}
    for name, (base, spread) in spreads.items():
        noise = np.random.default_rng([zlib.crc32(name.encode()), seed]).standard_normal(out[name].shape)
        drawn = base * np.exp(spread * noise) if base else spread * noise
        out[name] = jnp.asarray(drawn.astype(out[name].dtype))
    for name, factor in factors.items():
        out[name] = (out[name] * factor).astype(out[name].dtype)
    return out
```

```python
import concourse.bass as bass
from concourse import mybir
from contextlib import ExitStack

P = 128
CHUNKS = 5
EDGES = CHUNKS * P
SLOTS = 16
QUARTERS = 4
CAND = 8 * QUARTERS
LEVELS = 3
BITS = 8
TB = 4
BIG = 2.0 ** 53
LEAK = 0.2
EPS = 1e-5
LAG = 4
NEAR_LINKS, OWN_LINKS, KEY_LINKS = 2 * (LEVELS - 1) + 10, 6 + TB, 4
GW = P + 1


def constant_columns(n):
    at, out = 0, {}
    for name, width in (("ident", P), ("slot", CHUNKS * SLOTS), ("edge", CHUNKS),
                        ("before", P), ("position", EDGES), ("packed", n // BITS)):
        out[name] = (at, at + width)
        at += width
    return out, at


def constant_table(n):
    import numpy as np
    cols, width = constant_columns(n)
    IDX_BITS = (n // BITS).bit_length() - 1
    t = np.zeros((P, width), np.float32)

    def put(name, v):
        t[:, cols[name][0]:cols[name][1]] = v
    p = np.arange(P)
    put("ident", np.eye(P))
    put("before", p[:, None] < p[None, :])
    put("position", np.arange(EDGES)[None, :])
    put("slot", np.tile(np.arange(SLOTS), CHUNKS)[None, :])
    put("edge", p[:, None] + P * np.arange(CHUNKS)[None, :])
    m = np.arange(n // BITS)
    a, b = cols["packed"]
    t[0, a:b] = 2 ** (IDX_BITS - 1) * (2 ** BITS - 1)
    t[1, a:b] = m // 256 * 256
    t[2, a:b] = m % 256
    return t


def build(nc, x_in, adj, ks, w, a_vec, table, out):
    fp32, bf16, i32, f16 = mybir.dt.float32, mybir.dt.bfloat16, mybir.dt.int32, mybir.dt.float16
    ALU, ACT, AX = mybir.AluOpType, mybir.ActivationFunctionType, mybir.AxisListType
    N = x_in.shape[0]
    NT = N // P
    NB = NT // TB
    PW = N // BITS
    IDX_BITS = PW.bit_length() - 1
    HW = PW // 2
    QW = PW // QUARTERS
    KEY_PARTS = 2 * TB
    KEY_TILES = NT // KEY_PARTS
    PIECE = N // 4
    DC = 512
    DQ = DC // P
    ND = N // DC
    cols, table_w = constant_columns(N)
    ds = bass.ds

    x_rows = x_in.rearrange("(t p) d -> p t d", p=P)
    ks_rows = ks.rearrange("(t p) d -> p t d", p=P)
    adj_rows = adj.rearrange("(t p) m -> t p m", p=P)
    out_rows = out.rearrange("(t p) d -> t p d", p=P)

    ctx = ExitStack()
    with ctx:
        def sb(name, shape, dt):
            return ctx.enter_context(nc.sbuf_tensor(name, shape, dt))

        sems = {}

        def S(name):
            if name not in sems:
                sems[name] = ctx.enter_context(nc.semaphore(name))
            return sems[name]

        def linker(eng, name, turn, links):
            count = [0]

            def link(ins):
                count[0] += 1
                assert count[0] <= links, name
                ins.then_inc(S(name), 1)
                eng.wait_ge(S(name), turn * links + count[0])
                return count[0]
            link.count = count
            return link

        def settled(eng):
            eng.sem_inc(S(f"settled_{eng.engine.name}"), 1)

        def after(eng, name, value):
            if not isinstance(value, int) or value > 0:
                eng.wait_ge(S(name), value)

        kept_w = cols["edge"][1]
        const = sb("const", [P, kept_w], fp32)
        xs = sb("xs", [P, NT, P], fp32)
        keys = sb("keys", [P, KEY_TILES, P], fp32)
        key_part = sb("key_part", [P, P], fp32)
        adj_i = sb("adj_i", [P, 2, N], i32)
        adj_b = sb("adj_b", [P, 2, N], bf16)
        raw_const = adj_b[:, 1, :].bitcast(fp32)
        pack_w = sb("pack_w", [P, BITS, P], bf16)
        pack_c = sb("pack_c", [3, PW], bf16)
        ones3 = sb("ones3", [3, P], bf16)
        before = sb("before", [P, P], bf16)
        position = sb("position", [P, EDGES], f16)
        big_ident = sb("big_ident", [P, P], bf16)
        big_row = sb("big_row", [1, EDGES], bf16)
        half = sb("half", [P, 1], fp32)
        zero = sb("zero", [P, 1], fp32)
        eps = sb("eps", [P, 1], fp32)
        mean_w = sb("mean_w", [P, P], fp32)
        mean0 = sb("mean0", [P, P], fp32)
        mean1 = sb("mean1", [P, P], fp32)
        key_sum = sb("key_sum", [P, P], fp32)
        wext = sb("wext", [P, P + 2], fp32)
        w_t = sb("w_t", [P, P], fp32)
        a_col = sb("a_col", [P, 2], fp32)

        signs = sb("signs", [P, TB, 4], fp32)
        cand = sb("cand", [P, TB, LEVELS, CAND], fp32)
        top_bit = sb("top_bit", [P, 2, TB, CAND], fp32)
        cand_i = sb("cand_i", [P, 2, TB * LEVELS * CAND], i32)
        code_f = sb("code_f", [P, TB * LEVELS * CAND], fp32)
        code = sb("code", [P, TB, LEVELS * CAND], fp32)
        code2 = code_f[:, :].rearrange("p (t c) -> p t c", t=TB)
        near = sb("near", [P, TB, SLOTS + 1], fp32)
        is_near = sb("is_near", [P, TB, SLOTS], fp32)
        cnt = sb("cnt", [P, TB], fp32)
        cnt_b = sb("cnt_b", [P, TB], bf16)
        near_i = sb("near_i", [P, TB, SLOTS + 1], i32)
        split_i = sb("split_i", [P, TB, 2, SLOTS + 1], i32)
        split_b = sb("split_b", [P, TB, 2, SLOTS + 1], bf16)
        start_all = sb("start_all", [P, NT], fp32)
        end_all = sb("end_all", [P, NT], fp32)
        empty_all = sb("empty_all", [P, NT], fp32)
        some_all = sb("some_all", [P, NT], fp32)
        s_all = sb("s_all", [P, NT], fp32)
        from_start = sb("from_start", [P, 2, EDGES], bf16)
        own = sb("own", [P, 2 * TB, EDGES], bf16)
        my_slot = sb("my_slot", [P, TB, CHUNKS], fp32)
        pick = sb("pick", [P, TB, CHUNKS, SLOTS], fp32)
        key_f = sb("key_f", [P, TB, CHUNKS], fp32)
        key_idx = sb("key_idx", [P, NT * CHUNKS], i32)
        idx = sb("idx", [P, TB, CHUNKS], i32)
        deg = sb("deg", [P, 6, TB], fp32)
        bad = sb("bad", [P, 1], fp32)
        bad_n = sb("bad_n", [P, 2], fp32)
        flag = sb("flag", [1, 1], i32)

        stats = sb("stats", [P, TB, 6], fp32)
        mv = sb("mv", [P, TB, 2], fp32)
        lnv = sb("lnv", [P, TB], fp32)
        rstd = sb("rstd", [P, TB], fp32)
        nmr = sb("nmr", [P, TB], fp32)
        h = sb("h", [P, TB, P], fp32)
        h_t = sb("h_t", [P, 2, TB, P], fp32)
        g = sb("g", [P, TB, CHUNKS, GW], fp32)
        g_t = sb("g_t", [P, EDGES], fp32)
        neg_max = sb("neg_max", [P, 2], fp32)
        bias = sb("bias", [P, 2], fp32)
        leaky = sb("leaky", [P, EDGES], fp32)
        score = sb("score", [P, EDGES], fp32)
        prob = sb("prob", [P, EDGES], fp32)
        prob_t = sb("prob_t", [P, EDGES], fp32)
        prob_sum = sb("prob_sum", [P, 2], fp32)
        inv = sb("inv", [P, 2], fp32)
        inv_some = sb("inv_some", [P, 2], fp32)
        mixed = sb("mixed", [P, 2, P], fp32)
        below = sb("below", [P, 2, P], fp32)
        grown = sb("grown", [P, 2, P], fp32)
        above = sb("above", [P, 2, P], fp32)
        stats1 = sb("stats1", [P, 6], fp32)
        mv1 = sb("mv1", [P, 2], fp32)
        lnv1 = sb("lnv1", [P, 1], fp32)
        rstd1 = sb("rstd1", [P, 1], fp32)
        nmean1 = sb("nmean1", [P, 1], fp32)
        nmr1 = sb("nmr1", [P, 1], fp32)
        key_red = sb("key_red", [P, P], fp32)
        h1 = sb("h1", [P, P], fp32)
        h1_t = sb("h1_t", [P, P], fp32)
        g_out = sb("g_out", [P, 2, GW], fp32)
        dense_acc = h[:, 0, :]
        dense_sum = sb("dense_sum", [P, 1], fp32)
        dense_step = sb("dense_step", [P, 1], fp32)
        dense_keep = sb("dense_keep", [P, 1], fp32)
        y = sb("y", [P, 2, P], fp32)

        pk = ctx.enter_context(nc.psum_tensor("pk", [P, 2, 512], fp32))
        pl = ctx.enter_context(nc.psum_tensor("pl", [P, 2, 512], fp32))
        pt = ctx.enter_context(nc.psum_tensor("pt", [P, 1024], fp32))
        ps = ctx.enter_context(nc.psum_tensor("ps", [P, 1024], fp32))
        LW = CHUNKS * (SLOTS + 1)
        lists_ps = pl[:, 0, 0:TB * LW].rearrange("p (t c s) -> p t c s", t=TB, c=CHUNKS)
        starts_ps = pl[:, 0, TB * LW:TB * LW + TB]
        out_ps = pt[:, EDGES:EDGES + P]
        h1t_ps = pl[:, 1, 0:P]
        g_ps = pl[:, 1, P:2 * P + 2]
        mean_ps = pl[:, 1, 3 * P:4 * P]
        flag_ps = pl[0:1, 1, 3 * P:3 * P + 1]
        g_dram = nc.dram_tensor("layer1_keys", [N, GW], fp32)
        g_dram_cols = g_dram.ap().rearrange("(t p) d -> p t d", p=P)
        g_dram_rows = g_dram.ap().rearrange("(t p) d -> t p d", p=P)

        def c(name):
            a, b = cols[name]
            return const[:, a:b] if b <= kept_w else raw_const[:, a - kept_w:b - kept_w]

        ident = c("ident")
        cand_v = cand[:, :, :, :].rearrange("p t l c -> p (t l c)")
        cand_int = cand_v.bitcast(i32)
        parts = ((0, 512), (512, EDGES))

        block = ctx.enter_context(nc.Block())


        def holds(t, lo=0, hi=NT):
            return not isinstance(t, int) or lo <= t < hi

        def read_and_attend(eng, step):
            for j in range(4 * TB):
                step(j // TB, j % TB, j // TB % 2)
            with eng.Fori(4, NB, 2) as b:
                for j in range(2 * TB):
                    step(b + j // TB, j % TB, j // TB)
            for j in range(2 * TB + LAG):
                step(NB + j // TB, j % TB, j // TB % 2)

        def attend(eng, step):
            for j in range(2 * TB):
                step(j // TB, j % TB)
            with eng.Fori(2, NB) as b:
                for j in range(TB):
                    step(b, j)
            for j in range(LAG):
                step(NB, j)

        def row(ap, t):
            return ap[:, ds(t, 1), :].rearrange("p o d -> p (o d)")

        def dram_row(ap, t):
            return ap[ds(t, 1), :, :].rearrange("o p d -> p (o d)")


        def dense_turns(eng, layer, before_keys, on_keys, after_keys):
            with eng.Fori(0, NT) as t:
                u = t + NT * layer
                before_keys(t, u)
                with eng.Fori(0, ND) as k:
                    on_keys(t, u, k, u * ND + k)
                after_keys(t, u)

        def dense_sync(sp):
            sp.sem_inc(S("dense_g_stored"), 16)
            sp.sem_inc(S("dense_out_stored"), 16)
            sp.dma_start(xs[:, :, :], x_rows).then_inc(S("dense_x_in"), 16)
            for layer in range(2):
                def begin(t, u):
                    pass

                def load(t, u, k, v):
                    sp.wait_ge(S("dense_mixed"), v + 1)
                    sp.dma_start(adj_i[:, 0, 0:DC], dram_row(adj_rows, t)[:, ds(k * DC, DC)])\
                      .then_inc(S("dense_adj_in"), 16)
                    if layer == 0:
                        sp.dma_start(g[:, 0, 0:DQ, 0:P], ks_rows[:, ds(k * DQ, DQ), :]).then_inc(S("dense_keys_in"), 16)
                    else:
                        sp.dma_start(g[:, 0, 0:DQ, :], g_dram_cols[:, ds(k * DQ, DQ), :]).then_inc(S("dense_keys_in"), 16)

                def end(t, u):
                    if layer == 0:
                        sp.wait_ge(S("dense_g"), t + 1)
                        sp.dma_start(dram_row(g_dram_rows, t), g_out[:, 0, :]).then_inc(S("dense_g_stored"), 16)
                    else:
                        sp.wait_ge(S("dense_y"), t + 1)
                        sp.dma_start(dram_row(out_rows, t), y[:, 0, :]).then_inc(S("dense_out_stored"), 16)
                dense_turns(sp, layer, begin, load, end)
                if layer == 0:
                    sp.wait_ge(S("dense_g_stored"), 16 * NT + 16)
            sp.wait_ge(S("dense_out_stored"), 16 * NT + 16)

        def dense_act(act):
            def rows(t, n):
                act.wait_ge(S("dense_var"), n + 1)
                act.activation(lnv1[:, :], mv1[:, 1:2], ACT.Ln, bias=eps[:, 0:1]).then_inc(S("dense_ln"), 1)
                act.wait_ge(S("dense_ln"), n + 1)
                act.activation(rstd1[:, :], lnv1[:, :], ACT.Exp, scale=-0.5).then_inc(S("dense_rstd"), 1)
                act.wait_ge(S("dense_rstd"), n + 1)
                act.activation(nmr1[:, :], nmean1[:, :], ACT.Identity, scale=rstd1[:, 0:1]).then_inc(S("dense_nmr"), 1)
                act.wait_ge(S("dense_nmr"), n + 1)
                settled(act)
                act.activation(h1[:, :], row(xs, t), ACT.Relu, bias=nmr1[:, 0:1], scale=rstd1[:, 0:1])\
                   .then_inc(S("dense_h"), 1)

            for layer in range(2):
                def begin(t, u):
                    if layer == 0:
                        rows(t, 2 * t)

                def probs(t, u, k, v):
                    act.wait_ge(S("dense_scores"), v + 1)
                    settled(act)
                    act.activation(score[:, 0:DC], ps[:, 0:DC], ACT.Identity,
                                   bias=zero[:, 0:1] if layer == 0 else s_all[:, ds(t, 1)]).then_inc(S("dense_score"), 1)
                    act.wait_ge(S("dense_leaky"), v + 1)
                    act.activation(dense_keep[:, :], dense_step[:, :], ACT.Exp)
                    act.activation(prob[:, 0:DC], leaky[:, 0:DC], ACT.Exp, bias=bias[:, 0:1],
                                   accum_out=prob_sum[:, 0:1]).then_inc(S("dense_prob"), 1)

                def end(t, u):
                    if layer == 0:
                        rows(t, 2 * t + 1)
                    else:
                        act.wait_ge(S("dense_below"), t + 1)
                        act.activation(grown[:, 0, :], below[:, 0, :], ACT.Exp).then_inc(S("dense_grown"), 1)
                dense_turns(act, layer, begin, probs, end)

        def dense_pe(pe):
            pe.sem_inc(S("dense_mixed"), 1)

            def rows(n):
                pe.wait_ge(S("dense_h"), n + 1)
                pe.transpose(h1t_ps, h1[:, :], ident).then_inc(S("dense_h_t_ps"), 1)

            for layer in range(2):
                def begin(t, u):
                    if layer == 0:
                        rows(2 * t)
                        pe.wait_ge(S("dense_h_t"), 2 * t + 1)
                        settled(pe)

                def attend_keys(t, u, k, v):
                    pe.wait_ge(S("dense_keys_in"), 16 * v + 16)
                    pe.wait_ge(S("dense_taken"), v + 1)
                    if layer == 0:
                        for q in range(DQ):
                            last = pe.transpose(pt[:, q * P:(q + 1) * P], g[:, 0, q, 0:P], ident)
                        last.then_inc(S("dense_keys_t_ps"), 1)
                        pe.wait_ge(S("dense_keys_t"), v + 1)
                    pe.wait_ge(S("dense_own"), v + 1)
                    pe.matmul(ps[:, 0:DC], ones3[0:1, :], big_row[:, 0:DC], start=True, stop=False)
                    pe.matmul(ps[:, 0:DC], big_ident[:, :], own[:, 0, 0:DC], start=False, stop=False)
                    if layer == 0:
                        last = pe.matmul(ps[:, 0:DC], h1_t[:, :], g_t[:, 0:DC], start=False, stop=True)
                    else:
                        for q in range(DQ):
                            last = pe.matmul(ps[:, q * P:(q + 1) * P], g[:, 0, q, P:P + 1].to_broadcast([P, P]), ident,
                                             start=False, stop=q == DQ - 1)
                    last.then_inc(S("dense_scores"), 1)
                    pe.wait_ge(S("dense_prob"), v + 1)
                    for q in range(DQ):
                        last = pe.transpose(pt[:, q * P:(q + 1) * P], prob[:, q * P:(q + 1) * P], ident)
                    last.then_inc(S("dense_prob_t_ps"), 1)
                    pe.wait_ge(S("dense_prob_t"), v + 1)
                    for q in range(DQ):
                        last = pe.matmul(out_ps, prob_t[:, q * P:(q + 1) * P], g[:, 0, q, 0:P],
                                         start=q == 0, stop=q == DQ - 1)
                    last.then_inc(S("dense_mixed"), 1)

                def end(t, u):
                    if layer == 0:
                        rows(2 * t + 1)
                        pe.wait_ge(S("dense_h_t"), 2 * t + 2)
                        pe.matmul(g_ps, h1_t[:, :], wext[:, :], start=True, stop=True).then_inc(S("dense_g_ps"), 1)
                dense_turns(pe, layer, begin, attend_keys, end)

        def dense_dve(dve):
            TS, STT, TT = dve.tensor_scalar, dve.scalar_tensor_tensor, dve.tensor_tensor
            FAR = 1e38

            def rows(t, n):
                link = linker(dve, "dense_rows_step", n, 2)
                settled(dve)
                link(dve.bn_stats(stats1[:, :], row(xs, t)))
                settled(dve)
                link(dve.bn_aggr(mv1[:, :], stats1[:, :]))
                TS(nmean1[:, :], mv1[:, 0:1], -1.0, None, ALU.mult).then_inc(S("dense_var"), 1)
                dve.wait_ge(S("dense_h_t_ps"), n + 1)
                dve.tensor_copy(h1_t[:, :], h1t_ps).then_inc(S("dense_h_t"), 1)

            dve.sem_inc(S("dense_taken"), 1)
            dve.wait_ge(S("dense_x_in"), 16)
            for k in range(2):
                dve.wait_ge(S(f"g_stored{k}"), 16 * (NT // 2))
            for layer in range(2):
                def begin(t, u):
                    dve.wait_ge(S("dense_taken"), u * ND + 1)
                    dve.memset(dense_acc, 0.0)
                    dve.memset(dense_sum[:, :], 0.0)
                    dve.memset(bias[:, 1:2], FAR)
                    dve.memset(neg_max[:, 1:2], FAR).then_inc(S("dense_begun"), 1)
                    dve.wait_ge(S("dense_begun"), u + 1)
                    settled(dve)
                    if layer == 0:
                        rows(t, 2 * t)

                def soften(t, u, k, v):
                    link = linker(dve, "dense_step", v, 6)
                    dve.wait_ge(S("dense_adj_in"), 16 * v + 16)
                    TS(own[:, 0, 0:DC], adj_i[:, 0, 0:DC], 0.0, None, ALU.is_gt).then_inc(S("dense_own"), 1)
                    if layer == 0:
                        dve.wait_ge(S("dense_keys_t_ps"), v + 1)
                        dve.tensor_copy(g_t[:, 0:DC], pt[:, 0:DC]).then_inc(S("dense_keys_t"), 1)
                    dve.wait_ge(S("dense_score"), v + 1)
                    link(dve.tensor_reduce(neg_max[:, 0:1], score[:, 0:DC], AX.X, ALU.max, negate=True))
                    link(TT(neg_max[:, 1:2], neg_max[:, 0:1], neg_max[:, 1:2], ALU.min))
                    link(STT(bias[:, 0:1], neg_max[:, 1:2], LEAK, neg_max[:, 1:2], ALU.mult, ALU.min))
                    link(TT(dense_step[:, :], bias[:, 0:1], bias[:, 1:2], ALU.subtract))
                    dve.tensor_copy(bias[:, 1:2], bias[:, 0:1])
                    STT(leaky[:, 0:DC], score[:, 0:DC], LEAK, score[:, 0:DC], ALU.mult, ALU.max)\
                        .then_inc(S("dense_leaky"), 1)
                    dve.wait_ge(S("dense_prob_t_ps"), v + 1)
                    dve.tensor_copy(prob_t[:, 0:DC], pt[:, 0:DC]).then_inc(S("dense_prob_t"), 1)
                    dve.wait_ge(S("dense_mixed"), v + 2)
                    link(TT(dense_sum[:, :], dense_sum[:, :], dense_keep[:, :], ALU.mult))
                    link(TT(dense_sum[:, :], dense_sum[:, :], prob_sum[:, 0:1], ALU.add))
                    STT(dense_acc, dense_acc, dense_keep[:, 0:1], out_ps, ALU.mult, ALU.add)\
                        .then_inc(S("dense_taken"), 1)

                def end(t, u):
                    link = linker(dve, "dense_end_step", u, 2)
                    dve.wait_ge(S("dense_taken"), u * ND + ND + 1)
                    link(dve.reciprocal(inv[:, 0:1], dense_sum[:, :]))
                    if layer == 0:
                        link(STT(row(xs, t), dense_acc, inv[:, 0:1], row(xs, t), ALU.mult, ALU.add))
                        rows(t, 2 * t + 1)
                        dve.wait_ge(S("dense_g_ps"), t + 1)
                        dve.wait_ge(S("dense_g_stored"), 16 * t + 16)
                        dve.tensor_copy(s_all[:, ds(t, 1)], g_ps[:, GW:GW + 1])
                        dve.tensor_copy(g_out[:, 0, :], g_ps[:, 0:GW]).then_inc(S("dense_g"), 1)
                    else:
                        link(TS(mixed[:, 0, :], dense_acc, inv[:, 0:1], None, ALU.mult))
                        TS(below[:, 0, :], mixed[:, 0, :], 0.0, None, ALU.min).then_inc(S("dense_below"), 1)
                        STT(above[:, 0, :], mixed[:, 0, :], 0.0, row(xs, t), ALU.max, ALU.add).then_inc(S("dense_above"), 1)
                        dve.wait_ge(S("dense_grown"), t + 1)
                        dve.wait_ge(S("dense_above"), t + 1)
                        dve.wait_ge(S("dense_out_stored"), 16 * t + 16)
                        STT(y[:, 0, :], grown[:, 0, :], -1.0, above[:, 0, :], ALU.add, ALU.add).then_inc(S("dense_y"), 1)
                dense_turns(dve, layer, begin, soften, end)



        @block.sync
        def _(sp):
            sp.dma_start(const[:, :], table[:, 0:kept_w]).then_inc(S("const_in"), 16)
            sp.dma_start(raw_const[:, 0:table_w - kept_w], table[:, kept_w:table_w]).then_inc(S("raw_const_in"), 16)
            sp.dma_start(wext[:, 0:P], w).then_inc(S("w_in"), 16)
            with nc.allow_non_contiguous_dma("256 numbers"):
                sp.dma_start(a_col[:, :], a_vec.rearrange("(k p) o -> p (k o)", p=P)).then_inc(S("a_in"), 16)

            def load_adj(b, j):
                for hf in range(2):
                    lo = hf * (N // 2)
                    after(sp, "signs_done", 4 * (TB * b + j - 2) + 2 * hf + 2)
                    sp.dma_start(adj_i[:, j % 2, lo:lo + N // 2], dram_row(adj_rows, TB * b + j)[:, lo:lo + N // 2])\
                      .then_inc(S(f"adj_in{2 * (j % 2) + hf}"), 16)
            for j in range(TB):
                load_adj(0, j)
                if j == 1:
                    sp.dma_start(xs[:, :, :], x_rows).then_inc(S("x_in"), 16)
            with sp.Fori(1, NB) as b:
                for j in range(TB):
                    load_adj(b, j)

            sp.wait_ge(S("flag_ready"), 1)
            dense = sp.value_load(flag[0:1, 0:1], min_val=0, max_val=1)
            with sp.If(dense == 0):
                def store(b, j):
                    after(sp, "y_ready", TB * b + j + 1)
                    sp.dma_start(dram_row(out_rows, TB * b + j), y[:, j % 2, :]).then_inc(S(f"out_stored{j % 2}"), 16)
                with sp.Fori(0, NB) as b:
                    for j in range(TB):
                        store(b, j)
                for k in range(2):
                    sp.wait_ge(S(f"out_stored{k}"), 16 * (NT // 2))
            with sp.If(dense != 0):
                dense_sync(sp)

        @block.scalar
        def _(act):
            def sign_pieces(b, j, pieces):
                for q in pieces:
                    if q % 2 == 0:
                        act.wait_ge(S(f"adj_in{2 * (j % 2) + q // 2}"), 16 * (2 * b + j // 2 + 1))
                    if q == 0:
                        after(act, "packed", 2 * (TB * b + j - 2) + 2)
                        if j == 0:
                            after(act, "degree_read", b)
                    act.activation(adj_b[:, j % 2, q * PIECE:(q + 1) * PIECE],
                                   adj_i[:, j % 2, q * PIECE:(q + 1) * PIECE], ACT.Sign, bias=half[:, 0:1],
                                   accum_out=signs[:, j, q:q + 1]).then_inc(S("signs_done"), 1)

            def deviations(b):
                act.wait_ge(S("var0"), b + 1)
                act.activation(lnv[:, :], mv[:, :, 1], ACT.Ln, bias=eps[:, 0:1]).then_inc(S("lnv0"), 1)
                act.wait_ge(S("lnv0"), b + 1)
                act.activation(rstd[:, :], lnv[:, :], ACT.Exp, scale=-0.5).then_inc(S("rstd0"), 1)

            def rows_batch(b):
                act.wait_ge(S("nmr0"), b + 1)
                after(act, "h0_t_ps", b)
                settled(act)
                for j in range(TB):
                    act.activation(h[:, j, :], row(xs, b * TB + j), ACT.Relu,
                                   bias=nmr[:, j:j + 1], scale=rstd[:, j:j + 1]).then_inc(S("h0"), 1)

            def exp_tile(n, k):
                act.wait_ge(S("leaky"), n + 1)
                after(act, "prob_t_ps", n)
                act.activation(prob[:, :], leaky[:, :], ACT.Exp, bias=bias[:, k % 2:k % 2 + 1],
                               accum_out=prob_sum[:, k % 2:k % 2 + 1]).then_inc(S("prob"), 1)

            def rows_tile(t):
                act.wait_ge(S("var1"), t + 1)
                act.activation(lnv1[:, :], mv1[:, 1:2], ACT.Ln, bias=eps[:, 0:1]).then_inc(S("lnv1"), 1)
                act.wait_ge(S("lnv1"), t + 1)
                act.activation(rstd1[:, :], lnv1[:, :], ACT.Exp, scale=-0.5).then_inc(S("rstd1"), 1)
                act.wait_ge(S("rstd1"), t + 1)
                act.activation(nmr1[:, :], nmean1[:, :], ACT.Identity, scale=rstd1[:, 0:1]).then_inc(S("nmr1"), 1)
                act.wait_ge(S("nmr1"), t + 1)
                after(act, "h1_t_ps", t)
                settled(act)
                act.activation(h1[:, :], row(xs, t), ACT.Relu, bias=nmr1[:, 0:1], scale=rstd1[:, 0:1])\
                   .then_inc(S("h1"), 1)

            def store_g(t, k):
                act.wait_ge(S("g_out"), t + 1)
                act.dma_start(dram_row(g_dram_rows, t), g_out[:, k % 2, :]).then_inc(S(f"g_stored{k % 2}"), 16)

            def score_tile(n, row_part):
                act.wait_ge(S("scores"), n + 1)
                after(act, "leaky", n)
                act.activation(score[:, :], ps[:, 0:EDGES], ACT.Identity, bias=row_part).then_inc(S("score"), 1)

            act.wait_ge(S("act_consts"), 3)
            act.wait_ge(S("x_in"), 16)

            def step(b, j, par):
                t = TB * (b - 2) + j
                lb = b - 1
                reads, lists_it = holds(b, 0, NB), holds(lb, 0, NB)
                if isinstance(b, int) and b == 0 and j == 1:
                    act.wait_ge(S("dve_consts"), BITS + 4)
                if reads:
                    sign_pieces(b, j, (0, 1))
                if holds(t - 2):
                    exp_tile(t - 2, j - 2)
                if reads:
                    sign_pieces(b, j, (2,))
                if holds(t - 3):
                    rows_tile(t - 3)
                if reads:
                    sign_pieces(b, j, (3,))
                if holds(t - 1):
                    score_tile(t - 1, zero[:, 0:1])
                if holds(t - 4):
                    store_g(t - 4, j - 4)
                if lists_it and j == 1:
                    deviations(lb)
                if lists_it and j == 2:
                    rows_batch(lb)
            read_and_attend(act, step)

            act.wait_ge(S("flag_ready"), 1)
            dense = act.value_load(flag[0:1, 0:1], min_val=0, max_val=1)
            with act.If(dense == 0):
                def grow(t, k):
                    act.wait_ge(S("below"), t + 1)
                    after(act, "y_ready", t - 1)
                    act.activation(grown[:, k % 2, :], below[:, k % 2, :], ACT.Exp).then_inc(S("grown"), 1)

                def step1(b, j):
                    t = TB * b + j
                    if holds(t):
                        score_tile(NT + t, s_all[:, ds(t, 1)])
                    if holds(t - 1):
                        exp_tile(NT + t - 1, j - 1)
                    if holds(t - 3):
                        grow(t - 3, j - 3)
                attend(act, step1)
            with act.If(dense != 0):
                dense_act(act)

        @block.gpsimd
        def _(pool):
            pool.memset(half[:, :], -0.5).then_inc(S("act_consts"), 1)
            pool.memset(eps[:, :], EPS).then_inc(S("act_consts"), 1)
            pool.memset(zero[:, :], 0.0).then_inc(S("act_consts"), 1)
            pool.memset(ones3[:, :], 1.0).then_inc(S("pe_consts"), 1)
            pool.memset(big_row[:, :], -BIG).then_inc(S("pe_consts"), 1)
            pool.memset(mean_w[:, :], 1.0 / N).then_inc(S("pe_consts"), 1)

            for k in range(KEY_PARTS):
                after(pool, "key_red", k)
                pool.dma_start(keys[:, :, :], ks_rows[:, k * KEY_TILES:(k + 1) * KEY_TILES, :]).then_inc(S("keys_in"), 16)

            def gather(keys_ap, width, b, j, layer):
                t = TB * b + j
                n = NT * layer + t
                if layer == 0 and j == 0:
                    pool.wait_ge(S("keys_known"), b + 1)
                after(pool, f"g_in{j}", 16 * CHUNKS * (NB * layer + b))
                pool.tensor_copy(idx[:, j, :], key_idx[:, ds(CHUNKS * t, CHUNKS)]).then_inc(S("idx_ready"), 1)
                pool.wait_ge(S("idx_ready"), n + 1)
                after(pool, "mixed_ps", n - TB + 1)
                settled(pool)
                for q in range(CHUNKS):
                    pool.indirect_dma_start(g[:, j, q, 0:width], None, keys_ap,
                                            bass.IndirectOffsetOnAxis(ap=idx[:, j, q:q + 1], axis=0))\
                        .then_inc(S(f"g_in{j}"), 16)
            for j in range(TB):
                gather(ks, P, 0, j, 0)
            with pool.Fori(1, NB) as b:
                for j in range(TB):
                    gather(ks, P, b, j, 0)

            pool.wait_ge(S("flag_ready"), 1)
            dense = pool.value_load(flag[0:1, 0:1], min_val=0, max_val=1)
            with pool.If(dense == 0):
                for k in range(2):
                    pool.wait_ge(S(f"g_stored{k}"), 16 * (NT // 2))
                with pool.Fori(0, NB) as b:
                    for j in range(TB):
                        gather(g_dram.ap(), GW, b, j, 1)

        @block.tensor
        def _(pe):
            def mm(o, l, r, start=True, stop=True):
                return pe.matmul(o, l, r, start=start, stop=stop)

            def pack(b, j, bank):
                i = TB * b + j
                if bank == 0:
                    pe.wait_ge(S("signs_done"), 4 * i + 4)
                after(pe, "maxed", 2 * (i - 1) + bank + 1)
                lo = bank * HW
                mm(pk[:, bank, 0:HW], ones3[:, :], pack_c[:, lo:lo + HW], stop=False)
                for k in range(BITS):
                    last = mm(pk[:, bank, 0:HW], pack_w[:, k, :], adj_b[:, j % 2, k * PW + lo:k * PW + lo + HW],
                              start=False, stop=k == BITS - 1)
                last.then_inc(S("packed"), 1)

            def rows_batch(b):
                pe.wait_ge(S("h0"), TB * b + TB)
                pe.wait_ge(S("keys_known"), b + 1)
                for j in range(TB):
                    last = pe.transpose(pl[:, 0, j * P:(j + 1) * P], h[:, j, :], ident)
                last.then_inc(S("h0_t_ps"), 1)

            def starts(b):
                pe.wait_ge(S("cnt_ready"), b + 1)
                mm(starts_ps, before[:, :], cnt_b[:, :]).then_inc(S("starts_ps"), 1)

            def lists(b, par):
                pe.wait_ge(S("own_ready"), TB * b + TB)
                pe.wait_ge(S("split_ready"), b + 1)
                after(pe, "h0_t", b)
                for j in range(TB):
                    for q in range(CHUNKS):
                        for half_ in range(2):
                            last = mm(lists_ps[:, j, q, :], own[:, TB * par + j, q * P:(q + 1) * P], split_b[:, j, half_, :],
                                      start=half_ == 0, stop=half_ == 1)
                last.then_inc(S("listed_ps"), 1)

            def transpose_keys(b, j, t):
                pe.wait_ge(S(f"g_in{j}"), 16 * CHUNKS * (b + 1))
                after(pe, "prob_t", t - 1)
                for q in range(CHUNKS):
                    last = pe.transpose(pt[:, q * P:(q + 1) * P], g[:, j, q, 0:P], ident)
                last.then_inc(S("g_t_ps"), 1)

            def mask(n, j):
                for lo, hi in parts:
                    mm(ps[:, lo:hi], ones3[0:1, :], big_row[:, lo:hi], stop=False)
                    mm(ps[:, lo:hi], big_ident[:, :], own[:, j, lo:hi], start=False, stop=False)

            def scores0(t, j, par):
                pe.wait_ge(S("g_t"), t + 1)
                after(pe, "score", t)
                mask(t, TB * par + j)
                for lo, hi in parts:
                    last = mm(ps[:, lo:hi], h_t[:, par, j, :], g_t[:, lo:hi], start=False)
                last.then_inc(S("scores"), 1)

            def transpose_probs(n):
                pe.wait_ge(S("prob"), n + 1)
                after(pe, "out_read", n)
                for q in range(CHUNKS):
                    last = pe.transpose(pt[:, q * P:(q + 1) * P], prob[:, q * P:(q + 1) * P], ident)
                last.then_inc(S("prob_t_ps"), 1)

            def mix(n, k):
                pe.wait_ge(S("prob_t"), n + 1)
                for q in range(CHUNKS):
                    last = mm(out_ps, prob_t[:, q * P:(q + 1) * P], g[:, k % TB, q, 0:P],
                              start=q == 0, stop=q == CHUNKS - 1)
                last.then_inc(S("mixed_ps"), 1)

            def rows_tile(t):
                pe.wait_ge(S("h1"), t + 1)
                after(pe, "g_out", t)
                pe.transpose(h1t_ps, h1[:, :], ident).then_inc(S("h1_t_ps"), 1)

            def project(t):
                pe.wait_ge(S("h1_t"), t + 1)
                mm(g_ps, h1_t[:, :], wext[:, :]).then_inc(S("g_ps"), 1)

            pe.wait_ge(S("const_in"), 16)
            pe.wait_ge(S("w_in"), 16)
            pe.wait_ge(S("pe_consts"), 3)
            pe.transpose(pt[:, 0:P], wext[:, 0:P], ident).then_inc(S("w_t_ps"), 1)
            pe.wait_ge(S("a_in"), 16)
            pe.wait_ge(S("w_t"), 1)
            mm(ps[:, 0:2], w_t[:, :], a_col[:, :]).then_inc(S("wa_ps"), 1)
            pe.wait_ge(S("dve_consts"), BITS + 4)
            pe.wait_ge(S("wa"), 1)

            def step(b, j, par):
                t = TB * (b - 2) + j
                lb = b - 1
                reads, lists_it = holds(b, 0, NB), holds(lb, 0, NB)
                if holds(t - 4):
                    project(t - 4)
                if reads:
                    pack(b, j, 0)
                if holds(t - 2):
                    transpose_probs(t - 2)
                if holds(t):
                    transpose_keys(b - 2, j, t)
                if reads:
                    pack(b, j, 1)
                if holds(t - 2):
                    if holds(t):
                        pe.wait_ge(S("g_t"), t + 1)
                    mix(t - 2, j - 2)
                if holds(t):
                    scores0(t, j, par)
                if holds(t - 3):
                    rows_tile(t - 3)
                if lists_it and j == 0:
                    starts(lb)
                if lists_it and j == 1:
                    if isinstance(lb, int) and lb == 0:
                        pe.wait_ge(S("key_red"), KEY_PARTS)
                        mm(mean_ps, mean_w[:, :], key_red[:, :]).then_inc(S("mean0_ps"), 1)
                        pe.wait_ge(S("mean0"), 1)
                    lists(lb, 1 - par)
                if lists_it and j == 3:
                    rows_batch(lb)
            read_and_attend(pe, step)
            pe.wait_ge(S("bad_ready"), 1)
            mm(flag_ps, bad[:, 0:1], mean_w[:, 0:1]).then_inc(S("flag_ps"), 1)
            pe.wait_ge(S("g_out"), NT)
            pe.wait_ge(S("flag_ready"), 1)
            dense = pe.value_load(flag[0:1, 0:1], min_val=0, max_val=1)
            with pe.If(dense == 0):
                mm(mean_ps, mean_w[:, :], key_sum[:, :]).then_inc(S("mean1_ps"), 1)
                pe.wait_ge(S("mean1"), 1)

                def scores1(b, j):
                    t = TB * b + j
                    n = NT + t
                    pe.wait_ge(S("own_ready"), n + 1)
                    after(pe, "score", n)
                    mask(n, j)
                    pe.wait_ge(S(f"g_in{j}"), 16 * CHUNKS * (NB + b + 1))
                    for q in range(CHUNKS):
                        last = mm(ps[:, q * P:(q + 1) * P], g[:, j, q, P:P + 1].to_broadcast([P, P]), ident,
                                  start=False, stop=(q + 1) * P in (512, EDGES))
                    last.then_inc(S("scores"), 1)

                def step1(b, j):
                    t = TB * b + j
                    if holds(t):
                        scores1(b, j)
                    if holds(t - 2):
                        transpose_probs(NT + t - 2)
                        mix(NT + t - 2, j - 2)
                attend(pe, step1)
            with pe.If(dense != 0):
                dense_pe(pe)

        @block.vector
        def _(dve):
            TS, STT, TT = dve.tensor_scalar, dve.scalar_tensor_tensor, dve.tensor_tensor

            def top8(b, j, bank):
                dve.wait_ge(S("packed"), 2 * (TB * b + j) + bank + 1)
                settled(dve)
                for q in range(2):
                    o = 8 * (2 * bank + q)
                    last = dve.max(cand[:, j, 0, o:o + 8], pk[:, bank, q * QW:(q + 1) * QW])
                last.then_inc(S("maxed"), 1)

            def own_tile(k, t, link):
                link(TS(from_start[:, k % 2, :], position[:, :], start_all[:, ds(t, 1)], None, ALU.is_ge))
                STT(own[:, k, :], position[:, :], end_all[:, ds(t, 1)], from_start[:, k % 2, :], ALU.is_lt, ALU.mult)\
                    .then_inc(S("own_ready"), 1)

            def rows_batch(b):
                link = linker(dve, "rows_step", b, 1)
                settled(dve)
                for j in range(TB):
                    last = dve.bn_stats(stats[:, j, :], row(xs, TB * b + j))
                link(last)
                settled(dve)
                for j in range(TB):
                    last = dve.bn_aggr(mv[:, j, :], stats[:, j, :])
                last.then_inc(S("var0"), 1)

            def rows_shift(b):
                dve.wait_ge(S("var0"), b + 1)
                dve.wait_ge(S("rstd0"), b + 1)
                STT(nmr[:, :], mv[:, :, 0], -1.0, rstd[:, :], ALU.mult, ALU.mult).then_inc(S("nmr0"), 1)

            def near_rows(b):
                link = linker(dve, "near_step", b, NEAR_LINKS)
                dve.wait_ge(S("maxed"), 2 * TB * (b + 1))
                for lv in range(1, LEVELS):
                    above_v = cand[:, :, lv - 1, :]
                    tb = top_bit[:, lv - 1, :, :]
                    link(TS(tb.bitcast(i32), above_v.bitcast(i32), 0x7F800000, None, ALU.bitwise_and))
                    link(TT(cand[:, :, lv, :], above_v, tb, ALU.subtract))
                TS(cand_i[:, 1, :], cand_int, 23 - IDX_BITS, 255 << IDX_BITS, ALU.logical_shift_right, ALU.bitwise_and)
                link(dve.tensor_copy(cand_i[:, 0, :], cand_v))
                link(TS(cand_i[:, 0, :], cand_i[:, 0, :], (1 << IDX_BITS) - 1, None, ALU.bitwise_and))
                TS(code_f[:, :], cand_v, float(1 << IDX_BITS), None, ALU.is_ge)
                link(STT(cand_i[:, 0, :], cand_i[:, 1, :], float(1 - ((127 + IDX_BITS) << IDX_BITS)), cand_i[:, 0, :],
                         ALU.add, ALU.add))
                TT(code[:, :, :].rearrange("p t c -> p (t c)"), cand_i[:, 0, :], code_f[:, :], ALU.mult)\
                    .then_inc(S("coded"), 1)
                dve.wait_ge(S("coded"), b + 1)
                settled(dve)
                for j in range(TB):
                    last = dve.max(near[:, j, 0:8], code[:, j, :])
                link(last)
                settled(dve)
                for j in range(TB):
                    last = dve.match_replace(code2[:, j, :], near[:, j, 0:8], code[:, j, :], 0.0)
                link(last)
                settled(dve)
                for j in range(TB):
                    last = dve.max(near[:, j, 8:16], code2[:, j, :])
                link(last)
                link(TS(is_near[:, :, :], near[:, :, 0:SLOTS], 0.0, None, ALU.is_gt))
                link(dve.tensor_reduce(cnt[:, :], is_near[:, :, :], AX.X, ALU.add))
                dve.tensor_copy(cnt_b[:, :], cnt[:, :]).then_inc(S("cnt_ready"), 1)
                TS(empty_all[:, ds(TB * b, TB)], cnt[:, :], 0.0, None, ALU.is_equal)
                TS(some_all[:, ds(TB * b, TB)], cnt[:, :], 0.0, None, ALU.is_gt)
                dve.wait_ge(S("signs_done"), 4 * TB * (b + 1))
                dve.tensor_reduce(deg[:, 0, :], signs[:, :, :], AX.X, ALU.add).then_inc(S("degree_read"), 1)
                dve.wait_ge(S("degree_read"), b + 1)
                link(STT(deg[:, 1, :], cnt[:, :], 2.0, deg[:, 0, :], ALU.mult, ALU.subtract))
                link(TS(deg[:, 2, :], deg[:, 1, :], float(N), 0.0, ALU.subtract, ALU.not_equal))
                assert link.count[0] == NEAR_LINKS, link.count

            def own_runs(b, par):
                link = linker(dve, "own_step", b, OWN_LINKS)
                dve.wait_ge(S("starts_ps"), b + 1)
                dve.tensor_copy(near[:, :, SLOTS], starts_ps)
                dve.tensor_copy(start_all[:, ds(TB * b, TB)], starts_ps)
                link(TT(end_all[:, ds(TB * b, TB)], starts_ps, cnt[:, :], ALU.add))
                link(STT(deg[:, 3, :], end_all[:, ds(TB * b, TB)], float(EDGES), deg[:, 2, :], ALU.is_gt, ALU.add))
                link(dve.tensor_reduce(bad_n[:, 0:1], deg[:, 3, :], AX.X, ALU.add))
                link(TT(bad[:, :], bad[:, :], bad_n[:, 0:1], ALU.add))
                link(dve.tensor_copy(near_i[:, :, :], near[:, :, :]))
                TS(split_i[:, :, 0, :], near_i[:, :, :], 0x3FC0, None, ALU.bitwise_and)
                link(TS(split_i[:, :, 1, :], near_i[:, :, :], 63, None, ALU.bitwise_and))
                dve.tensor_copy(split_b[:, :, :, :], split_i[:, :, :, :]).then_inc(S("split_ready"), 1)
                after(dve, "scores", TB * (b - 1))
                for j in range(TB):
                    own_tile(TB * par + j, TB * b + j, link)
                assert link.count[0] == OWN_LINKS, link.count

            def rows_turned(b, par):
                dve.wait_ge(S("h0_t_ps"), b + 1)
                dve.tensor_copy(h_t[:, par, :, :].rearrange("p t d -> p (t d)"), pl[:, 0, :]).then_inc(S("h0_t"), 1)

            def edge_keys(b):
                link = linker(dve, "key_step", b, KEY_LINKS)
                dve.wait_ge(S("listed_ps"), b + 1)
                edge_b = c("edge").rearrange("p (t c) -> p t c", t=1).to_broadcast([P, TB, CHUNKS])
                link(TT(my_slot[:, :, :], edge_b, lists_ps[:, :, :, SLOTS], ALU.subtract))
                v3 = "p t c s -> p (t c) s"
                for j in range(TB):
                    last = TT(pick[:, j, :, :], c("slot").rearrange("p (c s) -> p c s", c=CHUNKS),
                              my_slot[:, j, :].rearrange("p (c o) -> p c o", o=1).to_broadcast([P, CHUNKS, SLOTS]), ALU.is_equal)
                link(last)
                link(TT(pick[:, :, :, :].rearrange(v3), pick[:, :, :, :].rearrange(v3),
                        lists_ps[:, :, :, 0:SLOTS].rearrange(v3), ALU.mult))
                link(dve.tensor_reduce(key_f[:, :, :].rearrange("p t c -> p (t c)"), pick[:, :, :, :].rearrange(v3), AX.X, ALU.add))
                TS(key_idx[:, ds(TB * CHUNKS * b, TB * CHUNKS)], key_f[:, :, :].rearrange("p t c -> p (t c)"), -1.0, 0.0,
                   ALU.add, ALU.max).then_inc(S("keys_known"), 1)
                assert link.count[0] == KEY_LINKS, link.count

            def keys_transposed(t):
                dve.wait_ge(S("g_t_ps"), t + 1)
                after(dve, "scores", t)
                dve.tensor_copy(g_t[:, :], pt[:, 0:EDGES]).then_inc(S("g_t"), 1)

            def soft(n, k):
                link = linker(dve, "soft_step", n, 1)
                dve.wait_ge(S("score"), n + 1)
                after(dve, "prob", n - 1)
                link(dve.tensor_reduce(neg_max[:, k % 2:k % 2 + 1], score[:, :], AX.X, ALU.max, negate=True))
                STT(bias[:, k % 2:k % 2 + 1], neg_max[:, k % 2:k % 2 + 1], LEAK, neg_max[:, k % 2:k % 2 + 1],
                    ALU.mult, ALU.min)
                after(dve, "prob", n)
                STT(leaky[:, :], score[:, :], LEAK, score[:, :], ALU.mult, ALU.max).then_inc(S("leaky"), 1)

            def probs_transposed(n):
                dve.wait_ge(S("prob_t_ps"), n + 1)
                after(dve, "mixed_ps", n)
                dve.tensor_copy(prob_t[:, :], pt[:, 0:EDGES]).then_inc(S("prob_t"), 1)

            def inverse(n, t, k):
                link = linker(dve, "inverse_step", n, 2)
                link(dve.reciprocal(inv[:, k % 2:k % 2 + 1], prob_sum[:, k % 2:k % 2 + 1]))
                link(TT(inv_some[:, k % 2:k % 2 + 1], inv[:, k % 2:k % 2 + 1], some_all[:, ds(t, 1)], ALU.mult))

            def output0(t, k):
                link = linker(dve, "output0_step", t, 3)
                dve.wait_ge(S("mixed_ps"), t + 1)
                inverse(t, t, k)
                STT(mixed[:, k % 2, :], out_ps, inv_some[:, k % 2:k % 2 + 1], row(xs, t), ALU.mult, ALU.add)\
                    .then_inc(S("out_read"), 1)
                dve.wait_ge(S("out_read"), t + 1)
                link(STT(row(xs, t), mean0[:, :], empty_all[:, ds(t, 1)], mixed[:, k % 2, :], ALU.mult, ALU.add))
                settled(dve)
                link(dve.bn_stats(stats1[:, :], row(xs, t)))
                after(dve, "h1", t)
                settled(dve)
                link(dve.bn_aggr(mv1[:, :], stats1[:, :]))
                TS(nmean1[:, :], mv1[:, 0:1], -1.0, None, ALU.mult).then_inc(S("var1"), 1)

            def rows_transposed(t):
                dve.wait_ge(S("h1_t_ps"), t + 1)
                after(dve, "g_ps", t)
                dve.tensor_copy(h1_t[:, :], h1t_ps).then_inc(S("h1_t"), 1)

            def keys1(t, b, j):
                dve.wait_ge(S("g_ps"), t + 1)
                if holds(t - 2):
                    dve.wait_ge(S(f"g_stored{j % 2}"), 16 * (2 * b + j // 2))
                dve.tensor_copy(s_all[:, ds(t, 1)], g_ps[:, GW:GW + 1])
                dve.tensor_copy(g_out[:, j % 2, :], g_ps[:, 0:GW]).then_inc(S("g_out"), 1)
                dve.wait_ge(S("g_out"), t + 1)
                TT(key_sum[:, :], key_sum[:, :], g_out[:, j % 2, 0:P], ALU.add).then_inc(S("key_sum"), 1)

            dve.memset(key_sum[:, :], 0.0).then_inc(S("zeroed"), 1)
            dve.memset(bad[:, :], 0.0).then_inc(S("zeroed"), 1)
            dve.memset(key_red[:, :], 0.0).then_inc(S("zeroed"), 1)
            dve.wait_ge(S("const_in"), 16)
            dve.wait_ge(S("raw_const_in"), 16)
            for k in range(BITS):
                TS(pack_w[:, k, :], ident, float(1 << (k + IDX_BITS - 1)), None, ALU.mult).then_inc(S("dve_consts"), 1)
            TS(big_ident[:, :], ident, BIG, None, ALU.mult).then_inc(S("dve_consts"), 1)
            dve.tensor_copy(before[:, :], c("before")).then_inc(S("dve_consts"), 1)
            dve.tensor_copy(pack_c[:, :], c("packed")[0:3, :]).then_inc(S("dve_consts"), 1)
            dve.tensor_copy(position[:, :], c("position")).then_inc(S("dve_consts"), 1)
            dve.wait_ge(S("w_t_ps"), 1)
            dve.tensor_copy(w_t[:, :], pt[:, 0:P]).then_inc(S("w_t"), 1)
            dve.wait_ge(S("wa_ps"), 1)
            dve.tensor_copy(wext[:, P:P + 1], ps[:, 1:2])
            dve.tensor_copy(wext[:, P + 1:P + 2], ps[:, 0:1]).then_inc(S("wa"), 1)
            dve.wait_ge(S("dve_consts"), BITS + 4)
            dve.wait_ge(S("zeroed"), 3)

            def step(b, j, par):
                t = TB * (b - 2) + j
                lb = b - 1
                reads, lists_it = holds(b, 0, NB), holds(lb, 0, NB)
                if lists_it and j == 0:
                    near_rows(lb)
                    if isinstance(lb, int) and lb == 0:
                        dve.wait_ge(S("x_in"), 16)
                    rows_batch(lb)
                if lists_it and j == 1:
                    own_runs(lb, 1 - par)
                if lists_it and j == 2:
                    edge_keys(lb)
                    rows_shift(lb)
                if holds(t - 4):
                    keys1(t - 4, b - 3, j)
                if reads:
                    top8(b, j, 0)
                if holds(t - 2):
                    probs_transposed(t - 2)
                if holds(t):
                    keys_transposed(t)
                if reads and isinstance(b, int) and b == 0:
                    for k in range(2 * j, 2 * j + 2):
                        dve.wait_ge(S("keys_in"), 16 * k + 16)
                        dve.tensor_reduce(key_part[:, :], keys[:, :, :].rearrange("p t d -> p d t"), AX.X, ALU.add)\
                            .then_inc(S("key_part"), 1)
                        dve.wait_ge(S("key_part"), k + 1)
                        after(dve, "key_red", k)
                        TT(key_red[:, :], key_red[:, :], key_part[:, :], ALU.add).then_inc(S("key_red"), 1)
                if reads:
                    top8(b, j, 1)
                if holds(t - 1):
                    soft(t - 1, j - 1)
                if holds(t - 2):
                    output0(t - 2, j - 2)
                if holds(t - 3):
                    rows_transposed(t - 3)
                if lists_it and j == 1 and isinstance(lb, int) and lb == 0:
                    dve.wait_ge(S("mean0_ps"), 1)
                    dve.tensor_copy(mean0[:, :], mean_ps).then_inc(S("mean0"), 1)
                    dve.wait_ge(S("mean0"), 1)
                if lists_it and j == 3:
                    rows_turned(lb, 1 - par)
            read_and_attend(dve, step)
            dve.wait_ge(S("own_step"), NB * OWN_LINKS)
            dve.memset(bad_n[:, 1:2], 1.0).then_inc(S("bad_ready"), 1)
            dve.wait_ge(S("flag_ps"), 1)
            TS(flag[:, :], flag_ps, 0.0, None, ALU.is_gt).then_inc(S("flag_ready"), 1)
            dve.wait_ge(S("flag_ready"), 1)
            dense = dve.value_load(flag[0:1, 0:1], min_val=0, max_val=1)
            with dve.If(dense == 0):
                dve.wait_ge(S("mean1_ps"), 1)
                dve.tensor_copy(mean1[:, :], mean_ps).then_inc(S("mean1"), 1)

                def mark(t, j):
                    link = linker(dve, "mark_step", t, 1)
                    after(dve, "scores", NT + t - TB + 1)
                    own_tile(j, t, link)

                def output1(t, k):
                    link = linker(dve, "output1_step", t, 1)
                    dve.wait_ge(S("mixed_ps"), NT + t + 1)
                    inverse(NT + t, t, k)
                    TS(above[:, k % 2, :], out_ps, inv_some[:, k % 2:k % 2 + 1], None, ALU.mult).then_inc(S("out_read"), 1)
                    dve.wait_ge(S("out_read"), NT + t + 1)
                    link(STT(mixed[:, k % 2, :], mean1[:, :], empty_all[:, ds(t, 1)], above[:, k % 2, :], ALU.mult, ALU.add))
                    TS(below[:, k % 2, :], mixed[:, k % 2, :], 0.0, None, ALU.min).then_inc(S("below"), 1)
                    STT(above[:, k % 2, :], mixed[:, k % 2, :], 0.0, row(xs, t), ALU.max, ALU.add).then_inc(S("above"), 1)

                def elu(t, b, j):
                    dve.wait_ge(S("grown"), t + 1)
                    dve.wait_ge(S("above"), t + 1)
                    if holds(t - 2):
                        dve.wait_ge(S(f"out_stored{j % 2}"), 16 * (2 * b + j // 2))
                    STT(y[:, j % 2, :], grown[:, j % 2, :], -1.0, above[:, j % 2, :], ALU.add, ALU.add).then_inc(S("y_ready"), 1)

                def step1(b, j):
                    t = TB * b + j
                    if holds(t):
                        mark(t, j)
                    if holds(t - 2):
                        probs_transposed(NT + t - 2)
                    if holds(t - 1):
                        soft(NT + t - 1, j - 1)
                    if holds(t - 2):
                        output1(t - 2, j - 2)
                    if holds(t - 3):
                        elu(t - 3, b if j >= 3 else b - 1, (j - 3) % TB)
                attend(dve, step1)
            with dve.If(dense != 0):
                dense_dve(dve)


def kernel(x, adj, L0_gnn_ks, L1_gnn_W, L1_gnn_a):
    import numpy as np
    import concourse.bacc as bacc
    from concourse.bass_utils import run_bass_kernel_spmd

    nc = bacc.Bacc("TRN2", target_bir_lowering=False, num_devices=1)
    arrays = {"x": x, "adj": adj, "ks": L0_gnn_ks, "w": L1_gnn_W, "a": L1_gnn_a, "table": constant_table(x.shape[0])}
    arrays = {name: np.ascontiguousarray(v) for name, v in arrays.items()}
    args = [nc.dram_tensor(name, v.shape, mybir.dt.from_np(v.dtype), kind="ExternalInput").ap()
            for name, v in arrays.items()]
    out = nc.dram_tensor("out", x.shape, mybir.dt.float32, kind="ExternalOutput").ap()
    build(nc, *args, out)
    return run_bass_kernel_spmd(nc, [arrays], core_ids=[0]).results[0]["out"]
```

```python
import concourse.bass as bass
from concourse import mybir
from contextlib import ExitStack

P = 128
CHUNKS = 5
EDGES = CHUNKS * P
SLOTS = 16
QUARTERS = 4
CAND = 8 * QUARTERS
LEVELS = 3
BITS = 8
TB = 4
BIG = 2.0 ** 53
LEAK = 0.2
EPS = 1e-5
LAG = 5
CODE_LINKS, NEAR_LINKS, OWN_LINKS, KEY_LINKS = 2 * (LEVELS - 1) + 3, 7, 6, 4
GW = P + 1


def constant_columns(n):
    at, out = 0, {}
    for name, width in (("ident", P), ("slot", CHUNKS * SLOTS), ("edge", CHUNKS),
                        ("before", P), ("position", EDGES), ("packed", n // BITS)):
        out[name] = (at, at + width)
        at += width
    return out, at


def constant_table(n):
    import numpy as np
    cols, width = constant_columns(n)
    IDX_BITS = (n // BITS).bit_length() - 1
    t = np.zeros((P, width), np.float32)

    def put(name, v):
        t[:, cols[name][0]:cols[name][1]] = v
    p = np.arange(P)
    put("ident", np.eye(P))
    put("before", p[:, None] < p[None, :])
    put("position", np.arange(EDGES)[None, :])
    put("slot", np.tile(np.arange(SLOTS), CHUNKS)[None, :])
    put("edge", p[:, None] + P * np.arange(CHUNKS)[None, :])
    m = np.arange(n // BITS)
    a, b = cols["packed"]
    t[0, a:b] = 2 ** (IDX_BITS - 1) * (2 ** BITS - 1)
    t[1, a:b] = m // 256 * 256
    t[2, a:b] = m % 256
    return t


def build(nc, x_in, adj, ks, w, a_vec, table, out):
    fp32, bf16, i32, f16 = mybir.dt.float32, mybir.dt.bfloat16, mybir.dt.int32, mybir.dt.float16
    ALU, ACT, AX = mybir.AluOpType, mybir.ActivationFunctionType, mybir.AxisListType
    N = x_in.shape[0]
    NT = N // P
    NB = NT // TB
    PW = N // BITS
    IDX_BITS = PW.bit_length() - 1
    HW = PW // 2
    QW = PW // QUARTERS
    KEY_PARTS = 2 * TB
    KEY_TILES = NT // KEY_PARTS
    PIECE = N // 4
    DC = 512
    DQ = DC // P
    ND = N // DC
    cols, table_w = constant_columns(N)
    ds = bass.ds

    x_rows = x_in.rearrange("(t p) d -> p t d", p=P)
    ks_rows = ks.rearrange("(t p) d -> p t d", p=P)
    adj_rows = adj.rearrange("(t p) m -> t p m", p=P)
    out_rows = out.rearrange("(t p) d -> t p d", p=P)

    ctx = ExitStack()
    with ctx:
        def sb(name, shape, dt):
            return ctx.enter_context(nc.sbuf_tensor(name, shape, dt))

        sems = {}

        def S(name):
            if name not in sems:
                sems[name] = ctx.enter_context(nc.semaphore(name))
            return sems[name]

        def linker(eng, name, turn, links):
            count = [0]

            def link(ins):
                count[0] += 1
                assert count[0] <= links, name
                ins.then_inc(S(name), 1)
                eng.wait_ge(S(name), turn * links + count[0])
                return count[0]
            link.count = count
            return link

        def settled(eng):
            eng.sem_inc(S(f"settled_{eng.engine.name}"), 1)

        def after(eng, name, value):
            if not isinstance(value, int) or value > 0:
                eng.wait_ge(S(name), value)

        kept_w = cols["edge"][1]
        const = sb("const", [P, kept_w], fp32)
        xs = sb("xs", [P, NT, P], fp32)
        key_part = sb("key_part", [P, P], fp32)
        adj_i = sb("adj_i", [P, 2, N], i32)
        adj_b = sb("adj_b", [P, 2, N], bf16)
        raw_const = adj_b[:, 1, :].bitcast(fp32)
        pack_w = sb("pack_w", [P, BITS, P], bf16)
        pack_c = sb("pack_c", [3, PW], bf16)
        ones3 = sb("ones3", [3, P], bf16)
        before = sb("before", [P, P], bf16)
        position = sb("position", [P, EDGES], f16)
        big_ident = sb("big_ident", [P, P], bf16)
        big_row = sb("big_row", [1, EDGES], bf16)
        half = sb("half", [P, 1], fp32)
        zero = sb("zero", [P, 1], fp32)
        eps = sb("eps", [P, 1], fp32)
        mean_w = sb("mean_w", [P, P], fp32)
        mean0 = sb("mean0", [P, P], fp32)
        mean1 = sb("mean1", [P, P], fp32)
        key_sum = sb("key_sum", [P, P], fp32)
        wext = sb("wext", [P, P + 2], fp32)
        w_t = sb("w_t", [P, P], fp32)
        a_col = sb("a_col", [P, 2], fp32)

        signs = sb("signs", [P, 2, TB, 4], fp32)
        cand = sb("cand", [P, TB, LEVELS, CAND], fp32)
        top_bit = sb("top_bit", [P, 2, TB, CAND], fp32)
        cand_i = sb("cand_i", [P, 2, TB * LEVELS * CAND], i32)
        code_f = sb("code_f", [P, TB * LEVELS * CAND], fp32)
        code = sb("code", [P, TB, LEVELS * CAND], fp32)
        code2 = code_f[:, :].rearrange("p (t c) -> p t c", t=TB)
        near = sb("near", [P, TB, SLOTS + 1], fp32)
        is_near = sb("is_near", [P, TB, SLOTS], fp32)
        cnt = sb("cnt", [P, TB], fp32)
        cnt_b = sb("cnt_b", [P, TB], bf16)
        near_i = sb("near_i", [P, TB, SLOTS + 1], i32)
        split_i = sb("split_i", [P, TB, 2, SLOTS + 1], i32)
        split_b = sb("split_b", [P, TB, 2, SLOTS + 1], bf16)
        start_all = sb("start_all", [P, NT], fp32)
        end_all = sb("end_all", [P, NT], fp32)
        until_end = sb("until_end", [P, TB, EDGES], bf16)
        empty_all = sb("empty_all", [P, NT], fp32)
        some_all = sb("some_all", [P, NT], fp32)
        s_all = sb("s_all", [P, NT], fp32)
        own = sb("own", [P, 2 * TB, EDGES], bf16)
        my_slot = sb("my_slot", [P, TB, CHUNKS], fp32)
        pick = sb("pick", [P, TB, CHUNKS, SLOTS], fp32)
        key_f = sb("key_f", [P, TB, CHUNKS], fp32)
        key_idx = sb("key_idx", [P, NT * CHUNKS], i32)
        idx = sb("idx", [P, TB, CHUNKS], i32)
        deg = sb("deg", [P, 6, TB], fp32)
        bad = sb("bad", [P, 1], fp32)
        bad_n = sb("bad_n", [P, 2], fp32)
        flag = sb("flag", [1, 1], i32)

        stats = sb("stats", [P, TB, 6], fp32)
        mv = sb("mv", [P, TB, 2], fp32)
        lnv = sb("lnv", [P, TB], fp32)
        rstd = sb("rstd", [P, TB], fp32)
        nmr = sb("nmr", [P, TB], fp32)
        h = sb("h", [P, TB, P], fp32)
        h_t = sb("h_t", [P, 2, TB, P], fp32)
        g = sb("g", [P, TB, CHUNKS, GW], fp32)
        keys = g[:, :, :, :].rearrange("p t c d -> p (t c d)")[:, 0:KEY_TILES * P]\
            .rearrange("p (t d) -> p t d", d=P)
        g_t = sb("g_t", [P, EDGES], fp32)
        neg_max = sb("neg_max", [P, 2], fp32)
        bias = sb("bias", [P, 2], fp32)
        leaky = sb("leaky", [P, EDGES], fp32)
        score = sb("score", [P, EDGES], fp32)
        prob = sb("prob", [P, EDGES], fp32)
        prob_t = sb("prob_t", [P, EDGES], fp32)
        prob_sum = sb("prob_sum", [P, 2], fp32)
        inv = sb("inv", [P, 2], fp32)
        inv_some = sb("inv_some", [P, 2], fp32)
        mixed = sb("mixed", [P, 2, P], fp32)
        below = sb("below", [P, 2, P], fp32)
        grown = sb("grown", [P, 2, P], fp32)
        above = sb("above", [P, 2, P], fp32)
        stats1 = sb("stats1", [P, 6], fp32)
        mv1 = sb("mv1", [P, 2], fp32)
        lnv1 = sb("lnv1", [P, 1], fp32)
        rstd1 = sb("rstd1", [P, 1], fp32)
        nmean1 = sb("nmean1", [P, 1], fp32)
        nmr1 = sb("nmr1", [P, 1], fp32)
        key_red = sb("key_red", [P, P], fp32)
        h1 = sb("h1", [P, P], fp32)
        h1_t = sb("h1_t", [P, P], fp32)
        g_out = sb("g_out", [P, 2, GW], fp32)
        dense_acc = h[:, 0, :]
        dense_sum = sb("dense_sum", [P, 1], fp32)
        dense_step = sb("dense_step", [P, 1], fp32)
        dense_keep = sb("dense_keep", [P, 1], fp32)
        y = sb("y", [P, 2, P], fp32)

        pk = ctx.enter_context(nc.psum_tensor("pk", [P, 2, 512], fp32))
        pl = ctx.enter_context(nc.psum_tensor("pl", [P, 2, 512], fp32))
        pt = ctx.enter_context(nc.psum_tensor("pt", [P, 1024], fp32))
        ps = ctx.enter_context(nc.psum_tensor("ps", [P, 1024], fp32))
        LW = CHUNKS * (SLOTS + 1)
        lists_ps = pl[:, 0, 0:TB * LW].rearrange("p (t c s) -> p t c s", t=TB, c=CHUNKS)
        starts_ps = pl[:, 0, TB * LW:TB * LW + TB]
        out_ps = pt[:, EDGES:EDGES + P]
        h1t_ps = pl[:, 1, 0:P]
        g_ps = pl[:, 1, P:2 * P + 2]
        mean_ps = pl[:, 1, 3 * P:4 * P]
        flag_ps = pl[0:1, 1, 3 * P:3 * P + 1]
        g_dram = nc.dram_tensor("layer1_keys", [N, GW], fp32)
        g_dram_cols = g_dram.ap().rearrange("(t p) d -> p t d", p=P)
        g_dram_rows = g_dram.ap().rearrange("(t p) d -> t p d", p=P)

        def c(name):
            a, b = cols[name]
            return const[:, a:b] if b <= kept_w else raw_const[:, a - kept_w:b - kept_w]

        ident = c("ident")
        cand_v = cand[:, :, :, :].rearrange("p t l c -> p (t l c)")
        cand_int = cand_v.bitcast(i32)
        parts = ((0, 512), (512, EDGES))

        block = ctx.enter_context(nc.Block())


        def holds(t, lo=0, hi=NT):
            return not isinstance(t, int) or lo <= t < hi

        def read_and_attend(eng, step):
            for j in range(4 * TB):
                step(j // TB, j % TB, j // TB % 2)
            with eng.Fori(4, NB, 2) as b:
                for j in range(2 * TB):
                    step(b + j // TB, j % TB, j // TB)
            for j in range(2 * TB + LAG):
                step(NB + j // TB, j % TB, j // TB % 2)

        def attend(eng, step):
            for j in range(2 * TB):
                step(j // TB, j % TB)
            with eng.Fori(2, NB) as b:
                for j in range(TB):
                    step(b, j)
            for j in range(3):
                step(NB, j)

        def pair(b, at):
            return TB // 2 * b + at // 2

        def row(ap, t):
            return ap[:, ds(t, 1), :].rearrange("p o d -> p (o d)")

        def dram_row(ap, t):
            return ap[ds(t, 1), :, :].rearrange("o p d -> p (o d)")


        def dense_turns(eng, layer, before_keys, on_keys, after_keys):
            with eng.Fori(0, NT) as t:
                u = t + NT * layer
                before_keys(t, u)
                with eng.Fori(0, ND) as k:
                    on_keys(t, u, k, u * ND + k)
                after_keys(t, u)

        def dense_sync(sp):
            sp.sem_inc(S("dense_g_stored"), 16)
            sp.sem_inc(S("dense_out_stored"), 16)
            sp.dma_start(xs[:, :, :], x_rows).then_inc(S("dense_x_in"), 16)
            for layer in range(2):
                def begin(t, u):
                    pass

                def load(t, u, k, v):
                    sp.wait_ge(S("dense_mixed"), v + 1)
                    sp.dma_start(adj_i[:, 0, 0:DC], dram_row(adj_rows, t)[:, ds(k * DC, DC)])\
                      .then_inc(S("dense_adj_in"), 16)
                    if layer == 0:
                        sp.dma_start(g[:, 0, 0:DQ, 0:P], ks_rows[:, ds(k * DQ, DQ), :]).then_inc(S("dense_keys_in"), 16)
                    else:
                        sp.dma_start(g[:, 0, 0:DQ, :], g_dram_cols[:, ds(k * DQ, DQ), :]).then_inc(S("dense_keys_in"), 16)

                def end(t, u):
                    if layer == 0:
                        sp.wait_ge(S("dense_g"), t + 1)
                        sp.dma_start(dram_row(g_dram_rows, t), g_out[:, 0, :]).then_inc(S("dense_g_stored"), 16)
                    else:
                        sp.wait_ge(S("dense_y"), t + 1)
                        sp.dma_start(dram_row(out_rows, t), y[:, 0, :]).then_inc(S("dense_out_stored"), 16)
                dense_turns(sp, layer, begin, load, end)
                if layer == 0:
                    sp.wait_ge(S("dense_g_stored"), 16 * NT + 16)
            sp.wait_ge(S("dense_out_stored"), 16 * NT + 16)

        def dense_act(act):
            def rows(t, n):
                act.wait_ge(S("dense_var"), n + 1)
                act.activation(lnv1[:, :], mv1[:, 1:2], ACT.Ln, bias=eps[:, 0:1]).then_inc(S("dense_ln"), 1)
                act.wait_ge(S("dense_ln"), n + 1)
                act.activation(rstd1[:, :], lnv1[:, :], ACT.Exp, scale=-0.5).then_inc(S("dense_rstd"), 1)
                act.wait_ge(S("dense_rstd"), n + 1)
                act.activation(nmr1[:, :], nmean1[:, :], ACT.Identity, scale=rstd1[:, 0:1]).then_inc(S("dense_nmr"), 1)
                act.wait_ge(S("dense_nmr"), n + 1)
                settled(act)
                act.activation(h1[:, :], row(xs, t), ACT.Relu, bias=nmr1[:, 0:1], scale=rstd1[:, 0:1])\
                   .then_inc(S("dense_h"), 1)

            for layer in range(2):
                def begin(t, u):
                    if layer == 0:
                        rows(t, 2 * t)

                def probs(t, u, k, v):
                    act.wait_ge(S("dense_scores"), v + 1)
                    settled(act)
                    act.activation(score[:, 0:DC], ps[:, 0:DC], ACT.Identity,
                                   bias=zero[:, 0:1] if layer == 0 else s_all[:, ds(t, 1)]).then_inc(S("dense_score"), 1)
                    act.wait_ge(S("dense_leaky"), v + 1)
                    act.activation(dense_keep[:, :], dense_step[:, :], ACT.Exp)
                    act.activation(prob[:, 0:DC], leaky[:, 0:DC], ACT.Exp, bias=bias[:, 0:1],
                                   accum_out=prob_sum[:, 0:1]).then_inc(S("dense_prob"), 1)

                def end(t, u):
                    if layer == 0:
                        rows(t, 2 * t + 1)
                    else:
                        act.wait_ge(S("dense_below"), t + 1)
                        act.activation(grown[:, 0, :], below[:, 0, :], ACT.Exp).then_inc(S("dense_grown"), 1)
                dense_turns(act, layer, begin, probs, end)

        def dense_pe(pe):
            pe.sem_inc(S("dense_mixed"), 1)

            def rows(n):
                pe.wait_ge(S("dense_h"), n + 1)
                pe.transpose(h1t_ps, h1[:, :], ident).then_inc(S("dense_h_t_ps"), 1)

            for layer in range(2):
                def begin(t, u):
                    if layer == 0:
                        rows(2 * t)
                        pe.wait_ge(S("dense_h_t"), 2 * t + 1)
                        settled(pe)

                def attend_keys(t, u, k, v):
                    pe.wait_ge(S("dense_keys_in"), 16 * v + 16)
                    pe.wait_ge(S("dense_taken"), v + 1)
                    if layer == 0:
                        for q in range(DQ):
                            last = pe.transpose(pt[:, q * P:(q + 1) * P], g[:, 0, q, 0:P], ident)
                        last.then_inc(S("dense_keys_t_ps"), 1)
                        pe.wait_ge(S("dense_keys_t"), v + 1)
                    pe.wait_ge(S("dense_own"), v + 1)
                    pe.matmul(ps[:, 0:DC], ones3[0:1, :], big_row[:, 0:DC], start=True, stop=False)
                    pe.matmul(ps[:, 0:DC], big_ident[:, :], own[:, 0, 0:DC], start=False, stop=False)
                    if layer == 0:
                        last = pe.matmul(ps[:, 0:DC], h1_t[:, :], g_t[:, 0:DC], start=False, stop=True)
                    else:
                        for q in range(DQ):
                            last = pe.matmul(ps[:, q * P:(q + 1) * P], g[:, 0, q, P:P + 1].to_broadcast([P, P]), ident,
                                             start=False, stop=q == DQ - 1)
                    last.then_inc(S("dense_scores"), 1)
                    pe.wait_ge(S("dense_prob"), v + 1)
                    for q in range(DQ):
                        last = pe.transpose(pt[:, q * P:(q + 1) * P], prob[:, q * P:(q + 1) * P], ident)
                    last.then_inc(S("dense_prob_t_ps"), 1)
                    pe.wait_ge(S("dense_prob_t"), v + 1)
                    for q in range(DQ):
                        last = pe.matmul(out_ps, prob_t[:, q * P:(q + 1) * P], g[:, 0, q, 0:P],
                                         start=q == 0, stop=q == DQ - 1)
                    last.then_inc(S("dense_mixed"), 1)

                def end(t, u):
                    if layer == 0:
                        rows(2 * t + 1)
                        pe.wait_ge(S("dense_h_t"), 2 * t + 2)
                        pe.matmul(g_ps, h1_t[:, :], wext[:, :], start=True, stop=True).then_inc(S("dense_g_ps"), 1)
                dense_turns(pe, layer, begin, attend_keys, end)

        def dense_dve(dve):
            TS, STT, TT = dve.tensor_scalar, dve.scalar_tensor_tensor, dve.tensor_tensor
            FAR = 1e38

            def rows(t, n):
                link = linker(dve, "dense_rows_step", n, 2)
                settled(dve)
                link(dve.bn_stats(stats1[:, :], row(xs, t)))
                settled(dve)
                link(dve.bn_aggr(mv1[:, :], stats1[:, :]))
                TS(nmean1[:, :], mv1[:, 0:1], -1.0, None, ALU.mult).then_inc(S("dense_var"), 1)
                dve.wait_ge(S("dense_h_t_ps"), n + 1)
                dve.tensor_copy(h1_t[:, :], h1t_ps).then_inc(S("dense_h_t"), 1)

            dve.sem_inc(S("dense_taken"), 1)
            dve.wait_ge(S("dense_x_in"), 16)
            for k in range(2):
                dve.wait_ge(S(f"g_stored{k}"), 16 * (NT // 2))
            for layer in range(2):
                def begin(t, u):
                    dve.wait_ge(S("dense_taken"), u * ND + 1)
                    dve.memset(dense_acc, 0.0)
                    dve.memset(dense_sum[:, :], 0.0)
                    dve.memset(bias[:, 1:2], FAR)
                    dve.memset(neg_max[:, 1:2], FAR).then_inc(S("dense_begun"), 1)
                    dve.wait_ge(S("dense_begun"), u + 1)
                    settled(dve)
                    if layer == 0:
                        rows(t, 2 * t)

                def soften(t, u, k, v):
                    link = linker(dve, "dense_step", v, 6)
                    dve.wait_ge(S("dense_adj_in"), 16 * v + 16)
                    TS(own[:, 0, 0:DC], adj_i[:, 0, 0:DC], 0.0, None, ALU.is_gt).then_inc(S("dense_own"), 1)
                    if layer == 0:
                        dve.wait_ge(S("dense_keys_t_ps"), v + 1)
                        dve.tensor_copy(g_t[:, 0:DC], pt[:, 0:DC]).then_inc(S("dense_keys_t"), 1)
                    dve.wait_ge(S("dense_score"), v + 1)
                    link(dve.tensor_reduce(neg_max[:, 0:1], score[:, 0:DC], AX.X, ALU.max, negate=True))
                    link(TT(neg_max[:, 1:2], neg_max[:, 0:1], neg_max[:, 1:2], ALU.min))
                    link(STT(bias[:, 0:1], neg_max[:, 1:2], LEAK, neg_max[:, 1:2], ALU.mult, ALU.min))
                    link(TT(dense_step[:, :], bias[:, 0:1], bias[:, 1:2], ALU.subtract))
                    dve.tensor_copy(bias[:, 1:2], bias[:, 0:1])
                    STT(leaky[:, 0:DC], score[:, 0:DC], LEAK, score[:, 0:DC], ALU.mult, ALU.max)\
                        .then_inc(S("dense_leaky"), 1)
                    dve.wait_ge(S("dense_prob_t_ps"), v + 1)
                    dve.tensor_copy(prob_t[:, 0:DC], pt[:, 0:DC]).then_inc(S("dense_prob_t"), 1)
                    dve.wait_ge(S("dense_mixed"), v + 2)
                    link(TT(dense_sum[:, :], dense_sum[:, :], dense_keep[:, :], ALU.mult))
                    link(TT(dense_sum[:, :], dense_sum[:, :], prob_sum[:, 0:1], ALU.add))
                    STT(dense_acc, dense_acc, dense_keep[:, 0:1], out_ps, ALU.mult, ALU.add)\
                        .then_inc(S("dense_taken"), 1)

                def end(t, u):
                    link = linker(dve, "dense_end_step", u, 2)
                    dve.wait_ge(S("dense_taken"), u * ND + ND + 1)
                    link(dve.reciprocal(inv[:, 0:1], dense_sum[:, :]))
                    if layer == 0:
                        link(STT(row(xs, t), dense_acc, inv[:, 0:1], row(xs, t), ALU.mult, ALU.add))
                        rows(t, 2 * t + 1)
                        dve.wait_ge(S("dense_g_ps"), t + 1)
                        dve.wait_ge(S("dense_g_stored"), 16 * t + 16)
                        dve.tensor_copy(s_all[:, ds(t, 1)], g_ps[:, GW:GW + 1])
                        dve.tensor_copy(g_out[:, 0, :], g_ps[:, 0:GW]).then_inc(S("dense_g"), 1)
                    else:
                        link(TS(mixed[:, 0, :], dense_acc, inv[:, 0:1], None, ALU.mult))
                        TS(below[:, 0, :], mixed[:, 0, :], 0.0, None, ALU.min).then_inc(S("dense_below"), 1)
                        STT(above[:, 0, :], mixed[:, 0, :], 0.0, row(xs, t), ALU.max, ALU.add).then_inc(S("dense_above"), 1)
                        dve.wait_ge(S("dense_grown"), t + 1)
                        dve.wait_ge(S("dense_above"), t + 1)
                        dve.wait_ge(S("dense_out_stored"), 16 * t + 16)
                        STT(y[:, 0, :], grown[:, 0, :], -1.0, above[:, 0, :], ALU.add, ALU.add).then_inc(S("dense_y"), 1)
                dense_turns(dve, layer, begin, soften, end)



        @block.sync
        def _(sp):
            sp.dma_start(const[:, :], table[:, 0:kept_w]).then_inc(S("const_in"), 16)
            sp.dma_start(raw_const[:, 0:table_w - kept_w], table[:, kept_w:table_w]).then_inc(S("raw_const_in"), 16)
            sp.dma_start(wext[:, 0:P], w).then_inc(S("w_in"), 16)
            with nc.allow_non_contiguous_dma("256 numbers"):
                sp.dma_start(a_col[:, :], a_vec.rearrange("(k p) o -> p (k o)", p=P)).then_inc(S("a_in"), 16)

            def load_adj(b, j):
                for hf in range(2):
                    lo = hf * (N // 2)
                    after(sp, "signs_done", 4 * (TB * b + j - 2) + 2 * hf + 2)
                    sp.dma_start(adj_i[:, j % 2, lo:lo + N // 2], dram_row(adj_rows, TB * b + j)[:, lo:lo + N // 2])\
                      .then_inc(S(f"adj_in{2 * (j % 2) + hf}"), 16)
            for j in range(TB):
                load_adj(0, j)
                if j == 1:
                    sp.dma_start(xs[:, :, :], x_rows).then_inc(S("x_in"), 16)
            with sp.Fori(1, NB) as b:
                for j in range(TB):
                    load_adj(b, j)

            sp.wait_ge(S("flag_ready"), 1)
            dense = sp.value_load(flag[0:1, 0:1], min_val=0, max_val=1)
            with sp.If(dense == 0):
                def store(b, j):
                    after(sp, "y_ready", TB * b + j + 1)
                    sp.dma_start(dram_row(out_rows, TB * b + j), y[:, j % 2, :]).then_inc(S(f"out_stored{j % 2}"), 16)
                with sp.Fori(0, NB) as b:
                    for j in range(TB):
                        store(b, j)
                for k in range(2):
                    sp.wait_ge(S(f"out_stored{k}"), 16 * (NT // 2))
            with sp.If(dense != 0):
                dense_sync(sp)

        @block.scalar
        def _(act):
            def sign_piece(b, j, par, q):
                if q % 2 == 0:
                    act.wait_ge(S(f"adj_in{2 * (j % 2) + q // 2}"), 16 * (2 * b + j // 2 + 1))
                if q == 0:
                    after(act, "packed", 2 * (TB * b + j - 2) + 2)
                    if j == 0:
                        after(act, "degree_read", b - 1)
                act.activation(adj_b[:, j % 2, q * PIECE:(q + 1) * PIECE],
                               adj_i[:, j % 2, q * PIECE:(q + 1) * PIECE], ACT.Sign, bias=half[:, 0:1],
                               accum_out=signs[:, par, j, q:q + 1]).then_inc(S("signs_done"), 1)

            def deviations(b):
                act.wait_ge(S("var0"), b + 1)
                act.activation(lnv[:, :], mv[:, :, 1], ACT.Ln, bias=eps[:, 0:1]).then_inc(S("lnv0"), 1)
                act.wait_ge(S("lnv0"), b + 1)
                act.activation(rstd[:, :], lnv[:, :], ACT.Exp, scale=-0.5).then_inc(S("rstd0"), 1)

            def rows_batch(b):
                act.wait_ge(S("nmr0"), b + 1)
                after(act, "h0_t_ps", b)
                settled(act)
                for j in range(TB):
                    act.activation(h[:, j, :], row(xs, b * TB + j), ACT.Relu,
                                   bias=nmr[:, j:j + 1], scale=rstd[:, j:j + 1]).then_inc(S("h0"), 1)

            def exp_tile(n, k):
                act.wait_ge(S("leaky"), n + 1)
                after(act, "prob_t_ps", n)
                act.activation(prob[:, :], leaky[:, :], ACT.Exp, bias=bias[:, k % 2:k % 2 + 1],
                               accum_out=prob_sum[:, k % 2:k % 2 + 1]).then_inc(S("prob"), 1)

            def rows_tile(t):
                act.wait_ge(S("var1"), t + 1)
                act.activation(lnv1[:, :], mv1[:, 1:2], ACT.Ln, bias=eps[:, 0:1]).then_inc(S("lnv1"), 1)
                act.wait_ge(S("lnv1"), t + 1)
                act.activation(rstd1[:, :], lnv1[:, :], ACT.Exp, scale=-0.5).then_inc(S("rstd1"), 1)
                act.wait_ge(S("rstd1"), t + 1)
                act.activation(nmr1[:, :], nmean1[:, :], ACT.Identity, scale=rstd1[:, 0:1]).then_inc(S("nmr1"), 1)
                act.wait_ge(S("nmr1"), t + 1)
                after(act, "h1_t_ps", t)
                settled(act)
                act.activation(h1[:, :], row(xs, t), ACT.Relu, bias=nmr1[:, 0:1], scale=rstd1[:, 0:1])\
                   .then_inc(S("h1"), 1)

            def store_g(t, k):
                act.wait_ge(S("g_out"), t + 1)
                act.dma_start(dram_row(g_dram_rows, t), g_out[:, k % 2, :]).then_inc(S(f"g_stored{k % 2}"), 16)

            def score_tile(n, row_part):
                act.wait_ge(S("scores"), n + 1)
                after(act, "leaky", n)
                act.activation(score[:, :], ps[:, 0:EDGES], ACT.Identity, bias=row_part).then_inc(S("score"), 1)

            act.preload_act_table_set("natural_log_exp_and_others")
            act.wait_ge(S("act_consts"), 3)
            act.wait_ge(S("x_in"), 16)

            def step(b, j, par):
                t = TB * b + j
                reads, lists_it = holds(b, 0, NB), holds(b - 1, 0, NB)
                if isinstance(b, int) and b == 0 and j == 1:
                    act.wait_ge(S("dve_consts"), BITS + 4)
                if reads:
                    sign_piece(b, j, par, 0)
                if lists_it and j == 2:
                    deviations(b - 1)
                if holds(t - 10):
                    exp_tile(t - 10, j - 10)
                if reads:
                    sign_piece(b, j, par, 1)
                if holds(t - 13):
                    store_g(t - 13, j - 13)
                if reads:
                    sign_piece(b, j, par, 2)
                if holds(t - 9):
                    score_tile(t - 9, zero[:, 0:1])
                if holds(t - 11):
                    rows_tile(t - 11)
                if reads:
                    sign_piece(b, j, par, 3)
                if lists_it and j == 3:
                    rows_batch(b - 1)
            read_and_attend(act, step)

            act.wait_ge(S("flag_ready"), 1)
            dense = act.value_load(flag[0:1, 0:1], min_val=0, max_val=1)
            with act.If(dense == 0):
                def grow(t, k):
                    act.wait_ge(S("below"), t + 1)
                    after(act, "y_ready", t - 1)
                    act.activation(grown[:, k % 2, :], below[:, k % 2, :], ACT.Exp).then_inc(S("grown"), 1)

                def step1(b, j):
                    t = TB * b + j
                    if holds(t):
                        score_tile(NT + t, s_all[:, ds(t, 1)])
                    if holds(t - 1):
                        exp_tile(NT + t - 1, j - 1)
                    if holds(t - 3):
                        grow(t - 3, j - 3)
                attend(act, step1)
            with act.If(dense != 0):
                dense_act(act)

        @block.gpsimd
        def _(pool):
            pool.memset(half[:, :], -0.5).then_inc(S("act_consts"), 1)
            pool.memset(eps[:, :], EPS).then_inc(S("act_consts"), 1)
            pool.memset(zero[:, :], 0.0).then_inc(S("act_consts"), 1)
            pool.memset(ones3[:, :], 1.0).then_inc(S("pe_consts"), 1)
            pool.memset(big_row[:, :], -BIG).then_inc(S("pe_consts"), 1)
            pool.memset(mean_w[:, :], 1.0 / N).then_inc(S("pe_consts"), 1)

            for k in range(KEY_PARTS):
                after(pool, "key_red", k)
                pool.dma_start(keys[:, :, :], ks_rows[:, k * KEY_TILES:(k + 1) * KEY_TILES, :]).then_inc(S("keys_in"), 16)

            def gather(keys_ap, width, b, j, layer):
                t = TB * b + j
                n = NT * layer + t
                if layer == 0 and j == 0:
                    pool.wait_ge(S("keys_known"), b + 1)
                after(pool, f"g_in{j}", 16 * CHUNKS * (NB * layer + b))
                pool.tensor_copy(idx[:, j, :], key_idx[:, ds(CHUNKS * t, CHUNKS)]).then_inc(S("idx_ready"), 1)
                pool.wait_ge(S("idx_ready"), n + 1)
                after(pool, "mixed_ps", n - TB + 1)
                settled(pool)
                for q in range(CHUNKS):
                    pool.indirect_dma_start(g[:, j, q, 0:width], None, keys_ap,
                                            bass.IndirectOffsetOnAxis(ap=idx[:, j, q:q + 1], axis=0))\
                        .then_inc(S(f"g_in{j}"), 16)

            def own_tile(k):
                pool.tensor_tensor(own[:, k, :], own[:, k, :], until_end[:, k % TB, :], ALU.mult).then_inc(S("own_ready"), 1)

            def step(b, j, par):
                if holds(b - 1, 0, NB) and j == 3:
                    pool.wait_ge(S("run_ends"), TB * (b - 1) + TB)
                    settled(pool)
                    for k in range(TB):
                        own_tile(TB * (1 - par) + k)
                if holds(TB * b + j - 7):
                    gather(ks, P, b + (j - 7) // TB, (j - 7) % TB, 0)
            read_and_attend(pool, step)

            pool.wait_ge(S("flag_ready"), 1)
            dense = pool.value_load(flag[0:1, 0:1], min_val=0, max_val=1)
            with pool.If(dense == 0):
                for k in range(2):
                    pool.wait_ge(S(f"g_stored{k}"), 16 * (NT // 2))
                with pool.Fori(0, NB) as b:
                    for j in range(TB):
                        gather(g_dram.ap(), GW, b, j, 1)

        @block.tensor
        def _(pe):
            def mm(o, l, r, start=True, stop=True):
                return pe.matmul(o, l, r, start=start, stop=stop)

            def pack(b, j, q):
                i = TB * b + j
                if q == 0:
                    after(pe, "maxed", 2 * i)
                    for bank in range(2):
                        mm(pk[:, bank, 0:HW], ones3[:, :], pack_c[:, bank * HW:(bank + 1) * HW], stop=False)
                pe.wait_ge(S("signs_done"), 4 * i + q + 1)
                per_piece = PIECE // PW
                for bank in range(2):
                    for k in range(per_piece * q, per_piece * (q + 1)):
                        lo = k * PW + bank * HW
                        last = mm(pk[:, bank, 0:HW], pack_w[:, k, :], adj_b[:, j % 2, lo:lo + HW],
                                  start=False, stop=k == BITS - 1)
                    if q == 3:
                        last.then_inc(S("packed"), 1)

            def rows_batch(b):
                pe.wait_ge(S("h0"), TB * b + TB)
                pe.wait_ge(S("keys_known"), b + 1)
                for j in range(TB):
                    last = pe.transpose(pl[:, 0, j * P:(j + 1) * P], h[:, j, :], ident)
                last.then_inc(S("h0_t_ps"), 1)

            def starts(b):
                pe.wait_ge(S("cnt_ready"), b + 1)
                after(pe, "h0_t", b)
                mm(starts_ps, before[:, :], cnt_b[:, :]).then_inc(S("starts_ps"), 1)

            def lists(b, par):
                pe.wait_ge(S("own_ready"), TB * b + TB)
                pe.wait_ge(S("split_ready"), b + 1)
                for j in range(TB):
                    for q in range(CHUNKS):
                        for half_ in range(2):
                            last = mm(lists_ps[:, j, q, :], own[:, TB * par + j, q * P:(q + 1) * P], split_b[:, j, half_, :],
                                      start=half_ == 0, stop=half_ == 1)
                last.then_inc(S("listed_ps"), 1)

            def transpose_keys(b, j, t):
                pe.wait_ge(S(f"g_in{j}"), 16 * CHUNKS * (b + 1))
                after(pe, "out_read", t - 1)
                for q in range(CHUNKS):
                    last = pe.transpose(pt[:, q * P:(q + 1) * P], g[:, j, q, 0:P], ident)
                last.then_inc(S("g_t_ps"), 1)

            def mask(n, j):
                for lo, hi in parts:
                    mm(ps[:, lo:hi], ones3[0:1, :], big_row[:, lo:hi], stop=False)
                    mm(ps[:, lo:hi], big_ident[:, :], own[:, j, lo:hi], start=False, stop=False)

            def scores0(t, k):
                pe.wait_ge(S("g_t"), t + 1)
                after(pe, "score", t)
                mask(t, k)
                for lo, hi in parts:
                    last = mm(ps[:, lo:hi], h_t[:, k // TB, k % TB, :], g_t[:, lo:hi], start=False)
                last.then_inc(S("scores"), 1)

            def transpose_probs(n):
                pe.wait_ge(S("prob"), n + 1)
                after(pe, "out_read", n)
                for q in range(CHUNKS):
                    last = pe.transpose(pt[:, q * P:(q + 1) * P], prob[:, q * P:(q + 1) * P], ident)
                last.then_inc(S("prob_t_ps"), 1)

            def mix(n, k):
                pe.wait_ge(S("prob_t"), n + 1)
                for q in range(CHUNKS):
                    last = mm(out_ps, prob_t[:, q * P:(q + 1) * P], g[:, k % TB, q, 0:P],
                              start=q == 0, stop=q == CHUNKS - 1)
                last.then_inc(S("mixed_ps"), 1)

            def rows_tile(t):
                pe.wait_ge(S("h1"), t + 1)
                after(pe, "g_out", t)
                pe.transpose(h1t_ps, h1[:, :], ident).then_inc(S("h1_t_ps"), 1)

            def project(t):
                pe.wait_ge(S("h1_t"), t + 1)
                mm(g_ps, h1_t[:, :], wext[:, :]).then_inc(S("g_ps"), 1)

            pe.wait_ge(S("const_in"), 16)
            pe.wait_ge(S("w_in"), 16)
            pe.wait_ge(S("pe_consts"), 3)
            pe.transpose(pt[:, 0:P], wext[:, 0:P], ident).then_inc(S("w_t_ps"), 1)
            pe.wait_ge(S("a_in"), 16)
            pe.wait_ge(S("w_t"), 1)
            mm(ps[:, 0:2], w_t[:, :], a_col[:, :]).then_inc(S("wa_ps"), 1)
            pe.wait_ge(S("dve_consts"), BITS + 4)
            pe.wait_ge(S("wa"), 1)

            def step(b, j, par):
                t = TB * b + j
                reads, lists_it = holds(b, 0, NB), holds(b - 1, 0, NB)
                if holds(t - 10):
                    pe.wait_ge(S("g_t"), min(t - 8, NT) if isinstance(t, int) else t - 8)
                    transpose_probs(t - 10)
                if holds(t - 9):
                    if j == 1:
                        pe.wait_ge(S("h0_t"), b - 1)
                    scores0(t - 9, (TB * par + j - 9) % (2 * TB))
                if reads:
                    pack(b, j, 0)
                if holds(t - 12):
                    project(t - 12)
                if lists_it and j == 1:
                    if isinstance(b, int) and b == 1:
                        pe.wait_ge(S("key_red"), KEY_PARTS)
                        mm(mean_ps, mean_w[:, :], key_red[:, :]).then_inc(S("mean0_ps"), 1)
                        pe.wait_ge(S("mean0"), 1)
                    starts(b - 1)
                if holds(t - 10):
                    mix(t - 10, j - 10)
                if reads:
                    pack(b, j, 1)
                    pack(b, j, 2)
                if holds(t - 11):
                    rows_tile(t - 11)
                if holds(t - 8):
                    transpose_keys(b - 2, j, t - 8)
                if lists_it and j == 3:
                    rows_batch(b - 1)
                if lists_it and j == 2:
                    lists(b - 1, 1 - par)
                if reads:
                    pack(b, j, 3)
            read_and_attend(pe, step)
            pe.wait_ge(S("bad_ready"), 1)
            mm(flag_ps, bad[:, 0:1], mean_w[:, 0:1]).then_inc(S("flag_ps"), 1)
            pe.wait_ge(S("g_out"), NT)
            pe.wait_ge(S("flag_ready"), 1)
            dense = pe.value_load(flag[0:1, 0:1], min_val=0, max_val=1)
            with pe.If(dense == 0):
                mm(mean_ps, mean_w[:, :], key_sum[:, :]).then_inc(S("mean1_ps"), 1)
                pe.wait_ge(S("mean1"), 1)

                def scores1(b, j):
                    t = TB * b + j
                    n = NT + t
                    pe.wait_ge(S("own_ready"), n + 1)
                    after(pe, "score", n)
                    mask(n, j)
                    pe.wait_ge(S(f"g_in{j}"), 16 * CHUNKS * (NB + b + 1))
                    for q in range(CHUNKS):
                        last = mm(ps[:, q * P:(q + 1) * P], g[:, j, q, P:P + 1].to_broadcast([P, P]), ident,
                                  start=False, stop=(q + 1) * P in (512, EDGES))
                    last.then_inc(S("scores"), 1)

                def step1(b, j):
                    t = TB * b + j
                    if holds(t):
                        scores1(b, j)
                    if holds(t - 2):
                        transpose_probs(NT + t - 2)
                        mix(NT + t - 2, j - 2)
                attend(pe, step1)
            with pe.If(dense != 0):
                dense_pe(pe)

        @block.vector
        def _(dve):
            TS, STT, TT = dve.tensor_scalar, dve.scalar_tensor_tensor, dve.tensor_tensor

            def top8(i, j, bank):
                dve.wait_ge(S("packed"), 2 * i + bank + 1)
                settled(dve)
                for q in range(2):
                    o = 8 * (2 * bank + q)
                    last = dve.max(cand[:, j, 0, o:o + 8], pk[:, bank, q * QW:(q + 1) * QW])
                last.then_inc(S("maxed"), 1)

            def run_starts(k, t):
                return TS(own[:, k, :], position[:, :], start_all[:, ds(t, 1)], None, ALU.is_ge)

            def rows_batch(b):
                link = linker(dve, "rows_step", b, 1)
                settled(dve)
                for j in range(TB):
                    last = dve.bn_stats(stats[:, j, :], row(xs, TB * b + j))
                link(last)
                settled(dve)
                for j in range(TB):
                    last = dve.bn_aggr(mv[:, j, :], stats[:, j, :])
                last.then_inc(S("var0"), 1)

            def rows_shift(b):
                dve.wait_ge(S("var0"), b + 1)
                dve.wait_ge(S("rstd0"), b + 1)
                STT(nmr[:, :], mv[:, :, 0], -1.0, rstd[:, :], ALU.mult, ALU.mult).then_inc(S("nmr0"), 1)

            def codes(b):
                link = linker(dve, "code_step", b, CODE_LINKS)
                dve.wait_ge(S("maxed"), 2 * TB * (b + 1))
                for lv in range(1, LEVELS):
                    above_v = cand[:, :, lv - 1, :]
                    tb = top_bit[:, lv - 1, :, :]
                    link(TS(tb.bitcast(i32), above_v.bitcast(i32), 0x7F800000, None, ALU.bitwise_and))
                    link(TT(cand[:, :, lv, :], above_v, tb, ALU.subtract))
                TS(cand_i[:, 1, :], cand_int, 23 - IDX_BITS, 255 << IDX_BITS, ALU.logical_shift_right, ALU.bitwise_and)
                link(dve.tensor_copy(cand_i[:, 0, :], cand_v))
                link(TS(cand_i[:, 0, :], cand_i[:, 0, :], (1 << IDX_BITS) - 1, None, ALU.bitwise_and))
                TS(code_f[:, :], cand_v, float(1 << IDX_BITS), None, ALU.is_ge)
                link(STT(cand_i[:, 0, :], cand_i[:, 1, :], float(1 - ((127 + IDX_BITS) << IDX_BITS)), cand_i[:, 0, :],
                         ALU.add, ALU.add))
                TT(code[:, :, :].rearrange("p t c -> p (t c)"), cand_i[:, 0, :], code_f[:, :], ALU.mult)\
                    .then_inc(S("coded"), 1)
                assert link.count[0] == CODE_LINKS, link.count

            def near_rows(b, par):
                link = linker(dve, "near_step", b, NEAR_LINKS)
                dve.wait_ge(S("coded"), b + 1)
                settled(dve)
                for j in range(TB):
                    last = dve.max(near[:, j, 0:8], code[:, j, :])
                link(last)
                settled(dve)
                for j in range(TB):
                    last = dve.match_replace(code2[:, j, :], near[:, j, 0:8], code[:, j, :], 0.0)
                link(last)
                settled(dve)
                for j in range(TB):
                    last = dve.max(near[:, j, 8:16], code2[:, j, :])
                link(last)
                link(TS(is_near[:, :, :], near[:, :, 0:SLOTS], 0.0, None, ALU.is_gt))
                link(dve.tensor_reduce(cnt[:, :], is_near[:, :, :], AX.X, ALU.add))
                dve.tensor_copy(cnt_b[:, :], cnt[:, :]).then_inc(S("cnt_ready"), 1)
                TS(empty_all[:, ds(TB * b, TB)], cnt[:, :], 0.0, None, ALU.is_equal)
                TS(some_all[:, ds(TB * b, TB)], cnt[:, :], 0.0, None, ALU.is_gt)
                dve.wait_ge(S("signs_done"), 4 * TB * (b + 1))
                dve.tensor_reduce(deg[:, 0, :], signs[:, par, :, :], AX.X, ALU.add).then_inc(S("degree_read"), 1)
                dve.wait_ge(S("degree_read"), b + 1)
                link(STT(deg[:, 1, :], cnt[:, :], 2.0, deg[:, 0, :], ALU.mult, ALU.subtract))
                link(TS(deg[:, 2, :], deg[:, 1, :], float(N), 0.0, ALU.subtract, ALU.not_equal))
                assert link.count[0] == NEAR_LINKS, link.count

            def own_runs(b, par):
                link = linker(dve, "own_step", b, OWN_LINKS)
                dve.wait_ge(S("starts_ps"), b + 1)
                dve.tensor_copy(near[:, :, SLOTS], starts_ps)
                dve.tensor_copy(start_all[:, ds(TB * b, TB)], starts_ps)
                link(TT(end_all[:, ds(TB * b, TB)], starts_ps, cnt[:, :], ALU.add))
                link(STT(deg[:, 3, :], end_all[:, ds(TB * b, TB)], float(EDGES), deg[:, 2, :], ALU.is_gt, ALU.add))
                link(dve.tensor_reduce(bad_n[:, 0:1], deg[:, 3, :], AX.X, ALU.add))
                link(TT(bad[:, :], bad[:, :], bad_n[:, 0:1], ALU.add))
                link(dve.tensor_copy(near_i[:, :, :], near[:, :, :]))
                TS(split_i[:, :, 0, :], near_i[:, :, :], 0x3FC0, None, ALU.bitwise_and)
                link(TS(split_i[:, :, 1, :], near_i[:, :, :], 63, None, ALU.bitwise_and))
                dve.tensor_copy(split_b[:, :, :, :], split_i[:, :, :, :]).then_inc(S("split_ready"), 1)
                after(dve, "scores", TB * (b - 1))
                for j in range(TB):
                    run_starts(TB * par + j, TB * b + j)
                    TS(until_end[:, j, :], position[:, :], end_all[:, ds(TB * b + j, 1)], None, ALU.is_lt)\
                        .then_inc(S("run_ends"), 1)
                assert link.count[0] == OWN_LINKS, link.count

            def rows_turned(b, par):
                dve.wait_ge(S("h0_t_ps"), b + 1)
                dve.tensor_copy(h_t[:, par, :, :].rearrange("p t d -> p (t d)"), pl[:, 0, :]).then_inc(S("h0_t"), 1)

            def edge_keys(b):
                link = linker(dve, "key_step", b, KEY_LINKS)
                dve.wait_ge(S("listed_ps"), b + 1)
                edge_b = c("edge").rearrange("p (t c) -> p t c", t=1).to_broadcast([P, TB, CHUNKS])
                link(TT(my_slot[:, :, :], edge_b, lists_ps[:, :, :, SLOTS], ALU.subtract))
                v3 = "p t c s -> p (t c) s"
                for j in range(TB):
                    last = TT(pick[:, j, :, :], c("slot").rearrange("p (c s) -> p c s", c=CHUNKS),
                              my_slot[:, j, :].rearrange("p (c o) -> p c o", o=1).to_broadcast([P, CHUNKS, SLOTS]), ALU.is_equal)
                link(last)
                link(TT(pick[:, :, :, :].rearrange(v3), pick[:, :, :, :].rearrange(v3),
                        lists_ps[:, :, :, 0:SLOTS].rearrange(v3), ALU.mult))
                link(dve.tensor_reduce(key_f[:, :, :].rearrange("p t c -> p (t c)"), pick[:, :, :, :].rearrange(v3), AX.X, ALU.add))
                TS(key_idx[:, ds(TB * CHUNKS * b, TB * CHUNKS)], key_f[:, :, :].rearrange("p t c -> p (t c)"), -1.0, 0.0,
                   ALU.add, ALU.max).then_inc(S("keys_known"), 1)
                assert link.count[0] == KEY_LINKS, link.count

            def keys_transposed(t):
                dve.wait_ge(S("g_t_ps"), t + 1)
                after(dve, "scores", t)
                dve.tensor_copy(g_t[:, :], pt[:, 0:EDGES]).then_inc(S("g_t"), 1)

            def soft(n, k):
                link = linker(dve, "soft_step", n, 1)
                dve.wait_ge(S("score"), n + 1)
                after(dve, "prob", n - 1)
                link(dve.tensor_reduce(neg_max[:, k % 2:k % 2 + 1], score[:, :], AX.X, ALU.max, negate=True))
                STT(bias[:, k % 2:k % 2 + 1], neg_max[:, k % 2:k % 2 + 1], LEAK, neg_max[:, k % 2:k % 2 + 1],
                    ALU.mult, ALU.min)
                after(dve, "prob", n)
                STT(leaky[:, :], score[:, :], LEAK, score[:, :], ALU.mult, ALU.max).then_inc(S("leaky"), 1)

            def probs_transposed(n):
                dve.wait_ge(S("prob_t_ps"), n + 1)
                after(dve, "mixed_ps", n)
                dve.tensor_copy(prob_t[:, :], pt[:, 0:EDGES]).then_inc(S("prob_t"), 1)

            def inverse(n, t, k):
                link = linker(dve, "inverse_step", n, 2)
                link(dve.reciprocal(inv[:, k % 2:k % 2 + 1], prob_sum[:, k % 2:k % 2 + 1]))
                link(TT(inv_some[:, k % 2:k % 2 + 1], inv[:, k % 2:k % 2 + 1], some_all[:, ds(t, 1)], ALU.mult))

            def output0(t, k):
                link = linker(dve, "output0_step", t, 3)
                dve.wait_ge(S("mixed_ps"), t + 1)
                inverse(t, t, k)
                STT(mixed[:, k % 2, :], out_ps, inv_some[:, k % 2:k % 2 + 1], row(xs, t), ALU.mult, ALU.add)\
                    .then_inc(S("out_read"), 1)
                dve.wait_ge(S("out_read"), t + 1)
                link(STT(row(xs, t), mean0[:, :], empty_all[:, ds(t, 1)], mixed[:, k % 2, :], ALU.mult, ALU.add))
                settled(dve)
                link(dve.bn_stats(stats1[:, :], row(xs, t)))
                after(dve, "h1", t)
                settled(dve)
                link(dve.bn_aggr(mv1[:, :], stats1[:, :]))
                TS(nmean1[:, :], mv1[:, 0:1], -1.0, None, ALU.mult).then_inc(S("var1"), 1)

            def rows_transposed(t):
                dve.wait_ge(S("h1_t_ps"), t + 1)
                after(dve, "g_ps", t)
                dve.tensor_copy(h1_t[:, :], h1t_ps).then_inc(S("h1_t"), 1)

            def keys1(t, b, j):
                dve.wait_ge(S("g_ps"), t + 1)
                if holds(t - 2):
                    dve.wait_ge(S(f"g_stored{j % 2}"), 16 * pair(b, j))
                dve.tensor_copy(s_all[:, ds(t, 1)], g_ps[:, GW:GW + 1])
                dve.tensor_copy(g_out[:, j % 2, :], g_ps[:, 0:GW]).then_inc(S("g_out"), 1)
                dve.wait_ge(S("g_out"), t + 1)
                TT(key_sum[:, :], key_sum[:, :], g_out[:, j % 2, 0:P], ALU.add).then_inc(S("key_sum"), 1)

            dve.memset(key_sum[:, :], 0.0).then_inc(S("zeroed"), 1)
            dve.memset(bad[:, :], 0.0).then_inc(S("zeroed"), 1)
            dve.memset(key_red[:, :], 0.0).then_inc(S("zeroed"), 1)
            dve.wait_ge(S("const_in"), 16)
            dve.wait_ge(S("raw_const_in"), 16)
            for k in range(BITS):
                TS(pack_w[:, k, :], ident, float(1 << (k + IDX_BITS - 1)), None, ALU.mult).then_inc(S("dve_consts"), 1)
            TS(big_ident[:, :], ident, BIG, None, ALU.mult).then_inc(S("dve_consts"), 1)
            dve.tensor_copy(before[:, :], c("before")).then_inc(S("dve_consts"), 1)
            dve.tensor_copy(pack_c[:, :], c("packed")[0:3, :]).then_inc(S("dve_consts"), 1)
            dve.tensor_copy(position[:, :], c("position")).then_inc(S("dve_consts"), 1)
            dve.wait_ge(S("w_t_ps"), 1)
            dve.tensor_copy(w_t[:, :], pt[:, 0:P]).then_inc(S("w_t"), 1)
            dve.wait_ge(S("wa_ps"), 1)
            dve.tensor_copy(wext[:, P:P + 1], ps[:, 1:2])
            dve.tensor_copy(wext[:, P + 1:P + 2], ps[:, 0:1]).then_inc(S("wa"), 1)
            dve.wait_ge(S("dve_consts"), BITS + 4)
            dve.wait_ge(S("zeroed"), 3)

            def step(b, j, par):
                t = TB * b + j
                lists_it = holds(b - 1, 0, NB)
                if holds(b - 2, 0, NB) and j == 0:
                    rows_turned(b - 2, par)
                if holds(t - 12):
                    rows_transposed(t - 12)
                if holds(t - 1):
                    for bank in range(2):
                        top8(t - 1, (j - 1) % TB, bank)
                if lists_it and j == 3:
                    rows_shift(b - 1)
                if lists_it and j == 0:
                    codes(b - 1)
                if lists_it and j == 1:
                    near_rows(b - 1, 1 - par)
                    if isinstance(b, int) and b == 1:
                        dve.wait_ge(S("x_in"), 16)
                    rows_batch(b - 1)
                if lists_it and j == 2:
                    own_runs(b - 1, 1 - par)
                if lists_it and j == 3:
                    edge_keys(b - 1)
                if holds(t - 10):
                    probs_transposed(t - 10)
                if holds(t - 12):
                    keys1(t - 12, b, j - 12)
                if holds(t - 9):
                    soft(t - 9, j - 9)
                if holds(t - 10):
                    output0(t - 10, j - 10)
                if holds(t - 8):
                    keys_transposed(t - 8)
                if isinstance(b, int) and b == 0:
                    for k in range(2 * j, 2 * j + 2):
                        dve.wait_ge(S("keys_in"), 16 * k + 16)
                        dve.tensor_reduce(key_part[:, :], keys[:, :, :].rearrange("p t d -> p d t"), AX.X, ALU.add)\
                            .then_inc(S("key_part"), 1)
                        dve.wait_ge(S("key_part"), k + 1)
                        after(dve, "key_red", k)
                        TT(key_red[:, :], key_red[:, :], key_part[:, :], ALU.add).then_inc(S("key_red"), 1)
                if isinstance(b, int) and b == 1 and j == 1:
                    dve.wait_ge(S("mean0_ps"), 1)
                    dve.tensor_copy(mean0[:, :], mean_ps).then_inc(S("mean0"), 1)
                    dve.wait_ge(S("mean0"), 1)
            read_and_attend(dve, step)
            dve.wait_ge(S("own_step"), NB * OWN_LINKS)
            dve.memset(bad_n[:, 1:2], 1.0).then_inc(S("bad_ready"), 1)
            dve.wait_ge(S("flag_ps"), 1)
            TS(flag[:, :], flag_ps, 0.0, None, ALU.is_gt).then_inc(S("flag_ready"), 1)
            dve.wait_ge(S("flag_ready"), 1)
            dense = dve.value_load(flag[0:1, 0:1], min_val=0, max_val=1)
            with dve.If(dense == 0):
                dve.wait_ge(S("mean1_ps"), 1)
                dve.tensor_copy(mean1[:, :], mean_ps).then_inc(S("mean1"), 1)

                def mark(t, j):
                    link = linker(dve, "mark_step", t, 1)
                    after(dve, "scores", NT + t - TB + 1)
                    link(run_starts(j, t))
                    STT(own[:, j, :], position[:, :], end_all[:, ds(t, 1)], own[:, j, :], ALU.is_lt, ALU.mult)\
                        .then_inc(S("own_ready"), 1)

                def output1(t, k):
                    link = linker(dve, "output1_step", t, 1)
                    dve.wait_ge(S("mixed_ps"), NT + t + 1)
                    inverse(NT + t, t, k)
                    TS(above[:, k % 2, :], out_ps, inv_some[:, k % 2:k % 2 + 1], None, ALU.mult).then_inc(S("out_read"), 1)
                    dve.wait_ge(S("out_read"), NT + t + 1)
                    link(STT(mixed[:, k % 2, :], mean1[:, :], empty_all[:, ds(t, 1)], above[:, k % 2, :], ALU.mult, ALU.add))
                    TS(below[:, k % 2, :], mixed[:, k % 2, :], 0.0, None, ALU.min).then_inc(S("below"), 1)
                    STT(above[:, k % 2, :], mixed[:, k % 2, :], 0.0, row(xs, t), ALU.max, ALU.add).then_inc(S("above"), 1)

                def elu(t, b, j):
                    dve.wait_ge(S("grown"), t + 1)
                    dve.wait_ge(S("above"), t + 1)
                    if holds(t - 2):
                        dve.wait_ge(S(f"out_stored{j % 2}"), 16 * (2 * b + j // 2))
                    STT(y[:, j % 2, :], grown[:, j % 2, :], -1.0, above[:, j % 2, :], ALU.add, ALU.add).then_inc(S("y_ready"), 1)

                def step1(b, j):
                    t = TB * b + j
                    if holds(t):
                        mark(t, j)
                    if holds(t - 2):
                        probs_transposed(NT + t - 2)
                    if holds(t - 1):
                        soft(NT + t - 1, j - 1)
                    if holds(t - 2):
                        output1(t - 2, j - 2)
                    if holds(t - 3):
                        elu(t - 3, b if j >= 3 else b - 1, (j - 3) % TB)
                attend(dve, step1)
            with dve.If(dense != 0):
                dense_dve(dve)


def kernel(x, adj, L0_gnn_ks, L1_gnn_W, L1_gnn_a):
    import numpy as np
    import concourse.bacc as bacc
    from concourse.bass_utils import run_bass_kernel_spmd

    nc = bacc.Bacc("TRN2", target_bir_lowering=False, num_devices=1)
    arrays = {"x": x, "adj": adj, "ks": L0_gnn_ks, "w": L1_gnn_W, "a": L1_gnn_a, "table": constant_table(x.shape[0])}
    arrays = {name: np.ascontiguousarray(v) for name, v in arrays.items()}
    args = [nc.dram_tensor(name, v.shape, mybir.dt.from_np(v.dtype), kind="ExternalInput").ap()
            for name, v in arrays.items()]
    out = nc.dram_tensor("out", x.shape, mybir.dt.float32, kind="ExternalOutput").ap()
    build(nc, *args, out)
    return run_bass_kernel_spmd(nc, [arrays], core_ids=[0]).results[0]["out"]
```

```python
import concourse.bass as bass
from concourse import mybir
from contextlib import ExitStack

P = 128
CHUNKS = 5
EDGES = CHUNKS * P
SLOTS = 16
QUARTERS = 4
CAND = 8 * QUARTERS
LEVELS = 3
BITS = 8
TB = 4
BIG = 2.0 ** 53
LEAK = 0.2
EPS = 1e-5
LAG = 7
CODE_LINKS, NEAR_LINKS, OWN_LINKS, KEY_LINKS = 2 * (LEVELS - 1) + 3, 7, 6, 4
GW = P + 1


def constant_columns(n):
    at, out = 0, {}
    for name, width in (("ident", P), ("slot", CHUNKS * SLOTS), ("edge", CHUNKS),
                        ("before", P), ("position", EDGES), ("packed", n // BITS)):
        out[name] = (at, at + width)
        at += width
    return out, at


def constant_table(n):
    import numpy as np
    cols, width = constant_columns(n)
    IDX_BITS = (n // BITS).bit_length() - 1
    t = np.zeros((P, width), np.float32)

    def put(name, v):
        t[:, cols[name][0]:cols[name][1]] = v
    p = np.arange(P)
    put("ident", np.eye(P))
    put("before", p[:, None] < p[None, :])
    put("position", np.arange(EDGES)[None, :])
    put("slot", np.tile(np.arange(SLOTS), CHUNKS)[None, :])
    put("edge", p[:, None] + P * np.arange(CHUNKS)[None, :])
    m = np.arange(n // BITS)
    a, b = cols["packed"]
    t[0, a:b] = 2 ** (IDX_BITS - 1) * (2 ** BITS - 1)
    t[1, a:b] = m // 256 * 256
    t[2, a:b] = m % 256
    return t


def build(nc, x_in, adj, ks, w, a_vec, table, out):
    fp32, bf16, i32, f16 = mybir.dt.float32, mybir.dt.bfloat16, mybir.dt.int32, mybir.dt.float16
    ALU, ACT, AX = mybir.AluOpType, mybir.ActivationFunctionType, mybir.AxisListType
    N = x_in.shape[0]
    NT = N // P
    NB = NT // TB
    PW = N // BITS
    IDX_BITS = PW.bit_length() - 1
    HW = PW // 2
    QW = PW // QUARTERS
    KEY_PARTS = 2
    KEY_TILES = NT // KEY_PARTS
    PIECE = N // 4
    DC = 512
    DQ = DC // P
    ND = N // DC
    cols, table_w = constant_columns(N)
    ds = bass.ds

    x_rows = x_in.rearrange("(t p) d -> p t d", p=P)
    ks_rows = ks.rearrange("(t p) d -> p t d", p=P)
    adj_rows = adj.rearrange("(t p) m -> t p m", p=P)
    out_rows = out.rearrange("(t p) d -> t p d", p=P)

    ctx = ExitStack()
    with ctx:
        def sb(name, shape, dt):
            return ctx.enter_context(nc.sbuf_tensor(name, shape, dt))

        sems = {}

        def S(name):
            if name not in sems:
                sems[name] = ctx.enter_context(nc.semaphore(name))
            return sems[name]

        def linker(eng, name, turn, links):
            count = [0]

            def link(ins):
                count[0] += 1
                assert count[0] <= links, name
                ins.then_inc(S(name), 1)
                eng.wait_ge(S(name), turn * links + count[0])
                return count[0]
            link.count = count
            return link

        def settled(eng):
            eng.sem_inc(S(f"settled_{eng.engine.name}"), 1)

        def after(eng, name, value):
            if not isinstance(value, int) or value > 0:
                eng.wait_ge(S(name), value)

        kept_w = cols["edge"][1]
        const = sb("const", [P, kept_w], fp32)
        xs = sb("xs", [P, NT, P], fp32)
        key_part = sb("key_part", [P, P], fp32)
        adj_i = sb("adj_i", [P, 2, N], i32)
        all_keys = adj_i[:, 1, :].bitcast(fp32).rearrange("p (t d) -> p t d", d=P)
        adj_b = sb("adj_b", [P, 2, N], bf16)
        raw_const = adj_b[:, 1, :].bitcast(fp32)
        pack_w = sb("pack_w", [P, BITS, P], bf16)
        pack_c = sb("pack_c", [3, PW], bf16)
        ones3 = sb("ones3", [3, P], bf16)
        before = sb("before", [P, P], bf16)
        position = sb("position", [P, EDGES], f16)
        big_ident = sb("big_ident", [P, P], bf16)
        big_row = sb("big_row", [2, EDGES], bf16)
        half = sb("half", [P, 1], fp32)
        zero = sb("zero", [P, 1], fp32)
        eps = sb("eps", [P, 1], fp32)
        mean_w = sb("mean_w", [P, P], fp32)
        mean0 = sb("mean0", [P, P], fp32)
        mean1 = sb("mean1", [P, P], fp32)
        key_sum = sb("key_sum", [P, P], fp32)
        wext = sb("wext", [P, P + 2], fp32)
        w_t = sb("w_t", [P, P], fp32)
        a_col = sb("a_col", [P, 2], fp32)

        signs = sb("signs", [P, 2, TB, 4], fp32)
        cand = sb("cand", [P, TB, LEVELS, CAND], fp32)
        top_bit = sb("top_bit", [P, 2, TB, CAND], fp32)
        cand_i = sb("cand_i", [P, 2, TB * LEVELS * CAND], i32)
        code_f = sb("code_f", [P, TB * LEVELS * CAND], fp32)
        code = sb("code", [P, TB, LEVELS * CAND], fp32)
        code2 = code_f[:, :].rearrange("p (t c) -> p t c", t=TB)
        near = sb("near", [P, TB, SLOTS + 1], fp32)
        is_near = sb("is_near", [P, TB, SLOTS], fp32)
        cnt = sb("cnt", [P, TB], fp32)
        cnt_b = sb("cnt_b", [P, TB], bf16)
        near_i = sb("near_i", [P, TB, SLOTS + 1], i32)
        split_i = sb("split_i", [P, TB, 2, SLOTS + 1], i32)
        split_b = sb("split_b", [P, TB, 2, SLOTS + 1], bf16)
        start_all = sb("start_all", [P, NT], fp32)
        end_all = sb("end_all", [P, NT], fp32)
        until_end = sb("until_end", [P, TB, EDGES], bf16)
        empty_all = sb("empty_all", [P, NT], fp32)
        some_all = sb("some_all", [P, NT], fp32)
        s_all = sb("s_all", [P, NT], fp32)
        own = sb("own", [P, 2 * TB, EDGES], bf16)
        my_slot = sb("my_slot", [P, TB, CHUNKS], fp32)
        pick = sb("pick", [P, TB, CHUNKS, SLOTS], fp32)
        key_f = sb("key_f", [P, TB, CHUNKS], fp32)
        key_idx = sb("key_idx", [P, NT * CHUNKS], i32)
        idx = sb("idx", [P, 2, TB, CHUNKS], i32)
        deg = sb("deg", [P, 6, TB], fp32)
        bad = sb("bad", [P, 1], fp32)
        bad_n = sb("bad_n", [P, 2], fp32)
        flag = sb("flag", [1, 1], i32)

        stats = sb("stats", [P, TB, 6], fp32)
        mv = sb("mv", [P, TB, 2], fp32)
        lnv = sb("lnv", [P, TB], fp32)
        rstd = sb("rstd", [P, TB], fp32)
        nmr = sb("nmr", [P, TB], fp32)
        h = sb("h", [P, TB, P], fp32)
        h_t = sb("h_t", [P, 2, TB, P], fp32)
        g = sb("g", [P, TB, CHUNKS, GW], fp32)
        g_t = sb("g_t", [P, EDGES], fp32)
        neg_max = sb("neg_max", [P, 2], fp32)
        bias = sb("bias", [P, 2], fp32)
        leaky = sb("leaky", [P, EDGES], fp32)
        score = sb("score", [P, EDGES], fp32)
        prob = sb("prob", [P, EDGES], fp32)
        prob_t = sb("prob_t", [P, EDGES], fp32)
        prob_sum = sb("prob_sum", [P, 2], fp32)
        inv = sb("inv", [P, 2], fp32)
        inv_some = sb("inv_some", [P, 2], fp32)
        mixed = sb("mixed", [P, 2, P], fp32)
        below = sb("below", [P, 2, P], fp32)
        grown = sb("grown", [P, 2, P], fp32)
        above = sb("above", [P, 2, P], fp32)
        stats1 = sb("stats1", [P, 6], fp32)
        mv1 = sb("mv1", [P, 2], fp32)
        lnv1 = sb("lnv1", [P, 1], fp32)
        rstd1 = sb("rstd1", [P, 1], fp32)
        nmean1 = sb("nmean1", [P, 1], fp32)
        nmr1 = sb("nmr1", [P, 1], fp32)
        key_red = sb("key_red", [P, P], fp32)
        h1 = sb("h1", [P, P], fp32)
        h1_t = sb("h1_t", [P, P], fp32)
        g_out = sb("g_out", [P, 2, GW], fp32)
        dense_acc = h[:, 0, :]
        dense_sum = sb("dense_sum", [P, 1], fp32)
        dense_step = sb("dense_step", [P, 1], fp32)
        dense_keep = sb("dense_keep", [P, 1], fp32)
        y = sb("y", [P, 2, P], fp32)

        pk = ctx.enter_context(nc.psum_tensor("pk", [P, 2, 512], fp32))
        pl = ctx.enter_context(nc.psum_tensor("pl", [P, 2, 512], fp32))
        pt = ctx.enter_context(nc.psum_tensor("pt", [P, 1024], fp32))
        ps = ctx.enter_context(nc.psum_tensor("ps", [P, 1024], fp32))
        LW = CHUNKS * (SLOTS + 1)
        lists_ps = pl[:, 0, 0:TB * LW].rearrange("p (t c s) -> p t c s", t=TB, c=CHUNKS)
        starts_ps = pl[:, 0, TB * LW:TB * LW + TB]
        out_ps = pt[:, EDGES:EDGES + P]
        out1_ps = pl[:, 0, 0:P]
        h1t_ps = pl[:, 1, 0:P]
        g_ps = pl[:, 1, P:2 * P + 2]
        mean_ps = pl[:, 1, 3 * P:4 * P]
        flag_ps = pl[0:1, 1, 3 * P:3 * P + 1]
        g_dram = nc.dram_tensor("layer1_keys", [N, GW], fp32)
        g_dram_cols = g_dram.ap().rearrange("(t p) d -> p t d", p=P)
        g_dram_rows = g_dram.ap().rearrange("(t p) d -> t p d", p=P)

        def c(name):
            a, b = cols[name]
            return const[:, a:b] if b <= kept_w else raw_const[:, a - kept_w:b - kept_w]

        ident = c("ident")
        cand_v = cand[:, :, :, :].rearrange("p t l c -> p (t l c)")
        cand_int = cand_v.bitcast(i32)
        parts = ((0, 512), (512, EDGES))

        block = ctx.enter_context(nc.Block())


        def holds(t, lo=0, hi=NT):
            return not isinstance(t, int) or lo <= t < hi

        def read_and_attend(eng, step):
            for j in range(4 * TB):
                step(j // TB, j % TB, j // TB % 2)
            with eng.Fori(4, NB, 2) as b:
                for j in range(2 * TB):
                    step(b + j // TB, j % TB, j // TB)
            for j in range(2 * TB + LAG):
                step(NB + j // TB, j % TB, j // TB % 2)

        def attend(eng, step):
            for j in range(2 * TB):
                step(j // TB, j % TB)
            with eng.Fori(2, NB) as b:
                for j in range(TB):
                    step(b, j)
            for j in range(3):
                step(NB, j)

        def pair(b, at):
            return TB // 2 * b + at // 2

        def row(ap, t):
            return ap[:, ds(t, 1), :].rearrange("p o d -> p (o d)")

        def dram_row(ap, t):
            return ap[ds(t, 1), :, :].rearrange("o p d -> p (o d)")


        def dense_turns(eng, layer, before_keys, on_keys, after_keys):
            with eng.Fori(0, NT) as t:
                u = t + NT * layer
                before_keys(t, u)
                with eng.Fori(0, ND) as k:
                    on_keys(t, u, k, u * ND + k)
                after_keys(t, u)

        def dense_sync(sp):
            sp.sem_inc(S("dense_g_stored"), 16)
            sp.sem_inc(S("dense_out_stored"), 16)
            sp.dma_start(xs[:, :, :], x_rows).then_inc(S("dense_x_in"), 16)
            for layer in range(2):
                def begin(t, u):
                    pass

                def load(t, u, k, v):
                    sp.wait_ge(S("dense_mixed"), v + 1)
                    sp.dma_start(adj_i[:, 0, 0:DC], dram_row(adj_rows, t)[:, ds(k * DC, DC)])\
                      .then_inc(S("dense_adj_in"), 16)
                    if layer == 0:
                        sp.dma_start(g[:, 0, 0:DQ, 0:P], ks_rows[:, ds(k * DQ, DQ), :]).then_inc(S("dense_keys_in"), 16)
                    else:
                        sp.dma_start(g[:, 0, 0:DQ, :], g_dram_cols[:, ds(k * DQ, DQ), :]).then_inc(S("dense_keys_in"), 16)

                def end(t, u):
                    if layer == 0:
                        sp.wait_ge(S("dense_g"), t + 1)
                        sp.dma_start(dram_row(g_dram_rows, t), g_out[:, 0, :]).then_inc(S("dense_g_stored"), 16)
                    else:
                        sp.wait_ge(S("dense_y"), t + 1)
                        sp.dma_start(dram_row(out_rows, t), y[:, 0, :]).then_inc(S("dense_out_stored"), 16)
                dense_turns(sp, layer, begin, load, end)
                if layer == 0:
                    sp.wait_ge(S("dense_g_stored"), 16 * NT + 16)
            sp.wait_ge(S("dense_out_stored"), 16 * NT + 16)

        def dense_act(act):
            def rows(t, n):
                act.wait_ge(S("dense_var"), n + 1)
                act.activation(lnv1[:, :], mv1[:, 1:2], ACT.Ln, bias=eps[:, 0:1]).then_inc(S("dense_ln"), 1)
                act.wait_ge(S("dense_ln"), n + 1)
                act.activation(rstd1[:, :], lnv1[:, :], ACT.Exp, scale=-0.5).then_inc(S("dense_rstd"), 1)
                act.wait_ge(S("dense_rstd"), n + 1)
                act.activation(nmr1[:, :], nmean1[:, :], ACT.Identity, scale=rstd1[:, 0:1]).then_inc(S("dense_nmr"), 1)
                act.wait_ge(S("dense_nmr"), n + 1)
                settled(act)
                act.activation(h1[:, :], row(xs, t), ACT.Relu, bias=nmr1[:, 0:1], scale=rstd1[:, 0:1])\
                   .then_inc(S("dense_h"), 1)

            for layer in range(2):
                def begin(t, u):
                    if layer == 0:
                        rows(t, 2 * t)

                def probs(t, u, k, v):
                    act.wait_ge(S("dense_scores"), v + 1)
                    settled(act)
                    act.activation(score[:, 0:DC], ps[:, 0:DC], ACT.Identity,
                                   bias=zero[:, 0:1] if layer == 0 else s_all[:, ds(t, 1)]).then_inc(S("dense_score"), 1)
                    act.wait_ge(S("dense_leaky"), v + 1)
                    act.activation(dense_keep[:, :], dense_step[:, :], ACT.Exp)
                    act.activation(prob[:, 0:DC], leaky[:, 0:DC], ACT.Exp, bias=bias[:, 0:1],
                                   accum_out=prob_sum[:, 0:1]).then_inc(S("dense_prob"), 1)

                def end(t, u):
                    if layer == 0:
                        rows(t, 2 * t + 1)
                    else:
                        act.wait_ge(S("dense_below"), t + 1)
                        act.activation(grown[:, 0, :], below[:, 0, :], ACT.Exp).then_inc(S("dense_grown"), 1)
                dense_turns(act, layer, begin, probs, end)

        def dense_pe(pe):
            pe.sem_inc(S("dense_mixed"), 1)

            def rows(n):
                pe.wait_ge(S("dense_h"), n + 1)
                pe.transpose(h1t_ps, h1[:, :], ident).then_inc(S("dense_h_t_ps"), 1)

            for layer in range(2):
                def begin(t, u):
                    if layer == 0:
                        rows(2 * t)
                        pe.wait_ge(S("dense_h_t"), 2 * t + 1)
                        settled(pe)

                def attend_keys(t, u, k, v):
                    pe.wait_ge(S("dense_keys_in"), 16 * v + 16)
                    pe.wait_ge(S("dense_taken"), v + 1)
                    if layer == 0:
                        for q in range(DQ):
                            last = pe.transpose(pt[:, q * P:(q + 1) * P], g[:, 0, q, 0:P], ident)
                        last.then_inc(S("dense_keys_t_ps"), 1)
                        pe.wait_ge(S("dense_keys_t"), v + 1)
                    pe.wait_ge(S("dense_own"), v + 1)
                    pe.matmul(ps[:, 0:DC], ones3[0:1, :], big_row[0:1, 0:DC], start=True, stop=False)
                    pe.matmul(ps[:, 0:DC], big_ident[:, :], own[:, 0, 0:DC], start=False, stop=False)
                    if layer == 0:
                        last = pe.matmul(ps[:, 0:DC], h1_t[:, :], g_t[:, 0:DC], start=False, stop=True)
                    else:
                        for q in range(DQ):
                            last = pe.matmul(ps[:, q * P:(q + 1) * P], g[:, 0, q, P:P + 1].to_broadcast([P, P]), ident,
                                             start=False, stop=q == DQ - 1)
                    last.then_inc(S("dense_scores"), 1)
                    pe.wait_ge(S("dense_prob"), v + 1)
                    for q in range(DQ):
                        last = pe.transpose(pt[:, q * P:(q + 1) * P], prob[:, q * P:(q + 1) * P], ident)
                    last.then_inc(S("dense_prob_t_ps"), 1)
                    pe.wait_ge(S("dense_prob_t"), v + 1)
                    for q in range(DQ):
                        last = pe.matmul(out_ps, prob_t[:, q * P:(q + 1) * P], g[:, 0, q, 0:P],
                                         start=q == 0, stop=q == DQ - 1)
                    last.then_inc(S("dense_mixed"), 1)

                def end(t, u):
                    if layer == 0:
                        rows(2 * t + 1)
                        pe.wait_ge(S("dense_h_t"), 2 * t + 2)
                        pe.matmul(g_ps, h1_t[:, :], wext[:, :], start=True, stop=True).then_inc(S("dense_g_ps"), 1)
                dense_turns(pe, layer, begin, attend_keys, end)

        def dense_dve(dve):
            TS, STT, TT = dve.tensor_scalar, dve.scalar_tensor_tensor, dve.tensor_tensor
            FAR = 1e38

            def rows(t, n):
                link = linker(dve, "dense_rows_step", n, 2)
                settled(dve)
                link(dve.bn_stats(stats1[:, :], row(xs, t)))
                settled(dve)
                link(dve.bn_aggr(mv1[:, :], stats1[:, :]))
                TS(nmean1[:, :], mv1[:, 0:1], -1.0, None, ALU.mult).then_inc(S("dense_var"), 1)
                dve.wait_ge(S("dense_h_t_ps"), n + 1)
                dve.tensor_copy(h1_t[:, :], h1t_ps).then_inc(S("dense_h_t"), 1)

            dve.sem_inc(S("dense_taken"), 1)
            dve.wait_ge(S("dense_x_in"), 16)
            for k in range(2):
                dve.wait_ge(S(f"g_stored{k}"), 16 * (NT // 2))
            for layer in range(2):
                def begin(t, u):
                    dve.wait_ge(S("dense_taken"), u * ND + 1)
                    dve.memset(dense_acc, 0.0)
                    dve.memset(dense_sum[:, :], 0.0)
                    dve.memset(bias[:, 1:2], FAR)
                    dve.memset(neg_max[:, 1:2], FAR).then_inc(S("dense_begun"), 1)
                    dve.wait_ge(S("dense_begun"), u + 1)
                    settled(dve)
                    if layer == 0:
                        rows(t, 2 * t)

                def soften(t, u, k, v):
                    link = linker(dve, "dense_step", v, 6)
                    dve.wait_ge(S("dense_adj_in"), 16 * v + 16)
                    TS(own[:, 0, 0:DC], adj_i[:, 0, 0:DC], 0.0, None, ALU.is_gt).then_inc(S("dense_own"), 1)
                    if layer == 0:
                        dve.wait_ge(S("dense_keys_t_ps"), v + 1)
                        dve.tensor_copy(g_t[:, 0:DC], pt[:, 0:DC]).then_inc(S("dense_keys_t"), 1)
                    dve.wait_ge(S("dense_score"), v + 1)
                    link(dve.tensor_reduce(neg_max[:, 0:1], score[:, 0:DC], AX.X, ALU.max, negate=True))
                    link(TT(neg_max[:, 1:2], neg_max[:, 0:1], neg_max[:, 1:2], ALU.min))
                    link(STT(bias[:, 0:1], neg_max[:, 1:2], LEAK, neg_max[:, 1:2], ALU.mult, ALU.min))
                    link(TT(dense_step[:, :], bias[:, 0:1], bias[:, 1:2], ALU.subtract))
                    dve.tensor_copy(bias[:, 1:2], bias[:, 0:1])
                    STT(leaky[:, 0:DC], score[:, 0:DC], LEAK, score[:, 0:DC], ALU.mult, ALU.max)\
                        .then_inc(S("dense_leaky"), 1)
                    dve.wait_ge(S("dense_prob_t_ps"), v + 1)
                    dve.tensor_copy(prob_t[:, 0:DC], pt[:, 0:DC]).then_inc(S("dense_prob_t"), 1)
                    dve.wait_ge(S("dense_mixed"), v + 2)
                    link(TT(dense_sum[:, :], dense_sum[:, :], dense_keep[:, :], ALU.mult))
                    link(TT(dense_sum[:, :], dense_sum[:, :], prob_sum[:, 0:1], ALU.add))
                    STT(dense_acc, dense_acc, dense_keep[:, 0:1], out_ps, ALU.mult, ALU.add)\
                        .then_inc(S("dense_taken"), 1)

                def end(t, u):
                    link = linker(dve, "dense_end_step", u, 2)
                    dve.wait_ge(S("dense_taken"), u * ND + ND + 1)
                    link(dve.reciprocal(inv[:, 0:1], dense_sum[:, :]))
                    if layer == 0:
                        link(STT(row(xs, t), dense_acc, inv[:, 0:1], row(xs, t), ALU.mult, ALU.add))
                        rows(t, 2 * t + 1)
                        dve.wait_ge(S("dense_g_ps"), t + 1)
                        dve.wait_ge(S("dense_g_stored"), 16 * t + 16)
                        dve.tensor_copy(s_all[:, ds(t, 1)], g_ps[:, GW:GW + 1])
                        dve.tensor_copy(g_out[:, 0, :], g_ps[:, 0:GW]).then_inc(S("dense_g"), 1)
                    else:
                        link(TS(mixed[:, 0, :], dense_acc, inv[:, 0:1], None, ALU.mult))
                        TS(below[:, 0, :], mixed[:, 0, :], 0.0, None, ALU.min).then_inc(S("dense_below"), 1)
                        STT(above[:, 0, :], mixed[:, 0, :], 0.0, row(xs, t), ALU.max, ALU.add).then_inc(S("dense_above"), 1)
                        dve.wait_ge(S("dense_grown"), t + 1)
                        dve.wait_ge(S("dense_above"), t + 1)
                        dve.wait_ge(S("dense_out_stored"), 16 * t + 16)
                        STT(y[:, 0, :], grown[:, 0, :], -1.0, above[:, 0, :], ALU.add, ALU.add).then_inc(S("dense_y"), 1)
                dense_turns(dve, layer, begin, soften, end)



        @block.sync
        def _(sp):
            sp.dma_start(const[:, :], table[:, 0:kept_w]).then_inc(S("const_in"), 16)
            packed_at = cols["packed"][0]
            sp.dma_start(raw_const[:, 0:packed_at - kept_w], table[:, kept_w:packed_at]).then_inc(S("raw_const_in"), 16)
            sp.dma_start(raw_const[0:3, packed_at - kept_w:table_w - kept_w], table[0:3, packed_at:table_w])\
              .then_inc(S("raw_const_in"), 16)
            sp.dma_start(wext[:, 0:P], w).then_inc(S("w_in"), 16)
            with nc.allow_non_contiguous_dma("256 numbers"):
                sp.dma_start(a_col[:, :], a_vec.rearrange("(k p) o -> p (k o)", p=P)).then_inc(S("a_in"), 16)

            for k in range(KEY_PARTS):
                sp.dma_start(all_keys[:, k * KEY_TILES:(k + 1) * KEY_TILES, :], ks_rows[:, k * KEY_TILES:(k + 1) * KEY_TILES, :])\
                  .then_inc(S(f"keys_in{k}"), 16)

            def load_adj(b, j):
                for hf in range(2):
                    lo = hf * (N // 2)
                    if isinstance(b, int) and b == 0 and j == 1:
                        sp.wait_ge(S("key_part"), hf + 1)
                    after(sp, "signs_done", 4 * (TB * b + j - 2) + 2 * hf + 2)
                    sp.dma_start(adj_i[:, j % 2, lo:lo + N // 2], dram_row(adj_rows, TB * b + j)[:, lo:lo + N // 2])\
                      .then_inc(S(f"adj_in{2 * (j % 2) + hf}"), 16)
            for j in range(TB):
                load_adj(0, j)
                if j == 1:
                    sp.dma_start(xs[:, :, :], x_rows).then_inc(S("x_in"), 16)
            with sp.Fori(1, NB) as b:
                for j in range(TB):
                    load_adj(b, j)

            sp.wait_ge(S("flag_ready"), 1)
            dense = sp.value_load(flag[0:1, 0:1], min_val=0, max_val=1)
            with sp.If(dense == 0):
                def store(b, j):
                    after(sp, "y_ready", TB * b + j + 1)
                    sp.dma_start(dram_row(out_rows, TB * b + j), y[:, j % 2, :]).then_inc(S(f"out_stored{j % 2}"), 16)
                with sp.Fori(0, NB) as b:
                    for j in range(TB):
                        store(b, j)
                for k in range(2):
                    sp.wait_ge(S(f"out_stored{k}"), 16 * (NT // 2))
            with sp.If(dense != 0):
                dense_sync(sp)

        @block.scalar
        def _(act):
            def sign_piece(b, j, par, q):
                if q % 2 == 0:
                    act.wait_ge(S(f"adj_in{2 * (j % 2) + q // 2}"), 16 * (2 * b + j // 2 + 1))
                if q == 0:
                    after(act, "packed", 2 * (TB * b + j - 2) + 2)
                    if j == 0:
                        after(act, "degree_read", b - 1)
                act.activation(adj_b[:, j % 2, q * PIECE:(q + 1) * PIECE],
                               adj_i[:, j % 2, q * PIECE:(q + 1) * PIECE], ACT.Sign, bias=half[:, 0:1],
                               accum_out=signs[:, par, j, q:q + 1]).then_inc(S("signs_done"), 1)

            def deviations(b):
                act.wait_ge(S("var0"), b + 1)
                act.activation(lnv[:, :], mv[:, :, 1], ACT.Ln, bias=eps[:, 0:1]).then_inc(S("lnv0"), 1)
                act.wait_ge(S("lnv0"), b + 1)
                act.activation(rstd[:, :], lnv[:, :], ACT.Exp, scale=-0.5).then_inc(S("rstd0"), 1)

            def rows_batch(b):
                act.wait_ge(S("nmr0"), b + 1)
                after(act, "h0_t_ps", b)
                settled(act)
                for j in range(TB):
                    act.activation(h[:, j, :], row(xs, b * TB + j), ACT.Relu,
                                   bias=nmr[:, j:j + 1], scale=rstd[:, j:j + 1]).then_inc(S("h0"), 1)

            def exp_tile(n, k):
                act.wait_ge(S("leaky"), n + 1)
                after(act, "prob_t_ps", n)
                act.activation(prob[:, :], leaky[:, :], ACT.Exp, bias=bias[:, k % 2:k % 2 + 1],
                               accum_out=prob_sum[:, k % 2:k % 2 + 1]).then_inc(S("prob"), 1)

            def rows_tile(t):
                act.wait_ge(S("var1"), t + 1)
                act.activation(lnv1[:, :], mv1[:, 1:2], ACT.Ln, bias=eps[:, 0:1]).then_inc(S("lnv1"), 1)
                act.wait_ge(S("lnv1"), t + 1)
                act.activation(rstd1[:, :], lnv1[:, :], ACT.Exp, scale=-0.5).then_inc(S("rstd1"), 1)
                act.wait_ge(S("rstd1"), t + 1)
                act.activation(nmr1[:, :], nmean1[:, :], ACT.Identity, scale=rstd1[:, 0:1]).then_inc(S("nmr1"), 1)
                act.wait_ge(S("nmr1"), t + 1)
                after(act, "h1_t_ps", t)
                settled(act)
                act.activation(h1[:, :], row(xs, t), ACT.Relu, bias=nmr1[:, 0:1], scale=rstd1[:, 0:1])\
                   .then_inc(S("h1"), 1)

            def store_g(t, k):
                act.wait_ge(S("g_out"), t + 1)
                act.dma_start(dram_row(g_dram_rows, t), g_out[:, k % 2, :]).then_inc(S(f"g_stored{k % 2}"), 16)

            def score_tile(n, row_part):
                act.wait_ge(S("scores"), n + 1)
                after(act, "leaky", n)
                act.activation(score[:, :], ps[:, 0:EDGES], ACT.Identity, bias=row_part).then_inc(S("score"), 1)

            act.preload_act_table_set("natural_log_exp_and_others")
            act.wait_ge(S("act_consts"), 3)

            def step(b, j, par):
                t = TB * b + j
                reads, lists_it = holds(b, 0, NB), holds(b - 1, 0, NB)
                if isinstance(b, int) and b == 0 and j == 1:
                    act.wait_ge(S("dve_consts"), BITS + 4)
                if reads:
                    sign_piece(b, j, par, 0)
                    sign_piece(b, j, par, 1)
                if holds(t - 13):
                    rows_tile(t - 13)
                if lists_it and j == 1:
                    deviations(b - 1)
                if holds(t - 10):
                    score_tile(t - 10, zero[:, 0:1])
                if lists_it and j == 2:
                    rows_batch(b - 1)
                if reads:
                    sign_piece(b, j, par, 2)
                    sign_piece(b, j, par, 3)
                if holds(t - 10):
                    exp_tile(t - 10, j - 10)
                if holds(t - 14):
                    store_g(t - 14, j - 14)
            read_and_attend(act, step)

            act.wait_ge(S("flag_ready"), 1)
            dense = act.value_load(flag[0:1, 0:1], min_val=0, max_val=1)
            with act.If(dense == 0):
                def grow(t, k):
                    act.wait_ge(S("below"), t + 1)
                    after(act, "y_ready", t - 1)
                    act.activation(grown[:, k % 2, :], below[:, k % 2, :], ACT.Exp).then_inc(S("grown"), 1)

                def probs_transposed(n):
                    act.wait_ge(S("prob_t_ps"), n + 1)
                    after(act, "mixed_ps", n)
                    act.activation(prob_t[:, :], pt[:, 0:EDGES], ACT.Identity, bias=zero[:, 0:1]).then_inc(S("prob_t"), 1)

                def step1(b, j):
                    t = TB * b + j
                    if holds(t - 1):
                        exp_tile(NT + t - 1, j - 1)
                    if holds(t):
                        score_tile(NT + t, s_all[:, ds(t, 1)])
                    if holds(t - 1):
                        probs_transposed(NT + t - 1)
                    if holds(t - 2):
                        grow(t - 2, j - 2)
                attend(act, step1)
            with act.If(dense != 0):
                dense_act(act)

        @block.gpsimd
        def _(pool):
            pool.memset(half[:, :], -0.5).then_inc(S("act_consts"), 1)
            pool.memset(eps[:, :], EPS).then_inc(S("act_consts"), 1)
            pool.memset(zero[:, :], 0.0).then_inc(S("act_consts"), 1)
            pool.memset(ones3[:, :], 1.0).then_inc(S("pe_consts"), 1)
            pool.memset(big_row[:, :], -BIG).then_inc(S("pe_consts"), 1)
            pool.memset(mean_w[:, :], 1.0 / N).then_inc(S("pe_consts"), 1)

            def gather(keys_ap, width, n, j, indices):
                after(pool, "mixed_ps", n - TB + 1)
                settled(pool)
                for q in range(CHUNKS):
                    pool.indirect_dma_start(g[:, j, q, 0:width], None, keys_ap,
                                            bass.IndirectOffsetOnAxis(ap=indices[:, q:q + 1], axis=0))\
                        .then_inc(S(f"g_in{j}"), 16)

            def gather0(b, j):
                t = TB * b + j
                if j == 0:
                    pool.wait_ge(S("keys_known"), b + 1)
                after(pool, f"g_in{j}", 16 * CHUNKS * b)
                pool.tensor_copy(idx[:, 0, j, :], key_idx[:, ds(CHUNKS * t, CHUNKS)]).then_inc(S("idx_ready"), 1)
                pool.wait_ge(S("idx_ready"), t + 1)
                gather(ks, P, t, j, idx[:, 0, j, :])

            def own_tile(k):
                pool.tensor_tensor(own[:, k, :], own[:, k, :], until_end[:, k % TB, :], ALU.mult).then_inc(S("own_ready"), 1)

            def sum_keys(t, k):
                pool.wait_ge(S("g_out"), t + 1)
                after(pool, "key_sum", t)
                pool.tensor_tensor(key_sum[:, :], key_sum[:, :], g_out[:, k % 2, 0:P], ALU.add).then_inc(S("key_sum"), 1)

            def step(b, j, par):
                t = TB * b + j
                if holds(t - 15):
                    sum_keys(t - 15, j - 15)
                if holds(t - 7):
                    gather0(b + (j - 7) // TB, (j - 7) % TB)
                if holds(b - 1, 0, NB) and j == 1:
                    pool.wait_ge(S("run_ends"), TB * (b - 1) + TB)
                    settled(pool)
                    for k in range(TB):
                        own_tile(TB * (1 - par) + k)
            read_and_attend(pool, step)

            pool.wait_ge(S("flag_ready"), 1)
            dense = pool.value_load(flag[0:1, 0:1], min_val=0, max_val=1)
            with pool.If(dense == 0):
                for k in range(2):
                    pool.wait_ge(S(f"g_stored{k}"), 16 * (NT // 2))
                with pool.Fori(0, NB // 2) as turn:
                    for par in range(2):
                        b = 2 * turn + par
                        for j in range(TB):
                            pool.wait_ge(S(f"g_in{j}"), 16 * CHUNKS * (b + NB - 1))
                        pool.tensor_copy(idx[:, par, :, :].rearrange("p t c -> p (t c)"),
                                         key_idx[:, ds(TB * CHUNKS * b, TB * CHUNKS)]).then_inc(S("idx_ready"), 1)
                        pool.wait_ge(S("idx_ready"), b + NT + 1)
                        for j in range(TB):
                            gather(g_dram.ap(), GW, TB * b + j + NT, j, idx[:, par, j, :])

        @block.tensor
        def _(pe):
            def mm(o, l, r, start=True, stop=True):
                return pe.matmul(o, l, r, start=start, stop=stop)

            def pack(b, j, q):
                i = TB * b + j
                if q == 0:
                    after(pe, "maxed", 2 * i)
                    for bank in range(2):
                        mm(pk[:, bank, 0:HW], ones3[:, :], pack_c[:, bank * HW:(bank + 1) * HW], stop=False)
                pe.wait_ge(S("signs_done"), 4 * i + q + 1)
                per_piece = PIECE // PW
                for bank in range(2):
                    for k in range(per_piece * q, per_piece * (q + 1)):
                        lo = k * PW + bank * HW
                        last = mm(pk[:, bank, 0:HW], pack_w[:, k, :], adj_b[:, j % 2, lo:lo + HW],
                                  start=False, stop=k == BITS - 1)
                    if q == 3:
                        last.then_inc(S("packed"), 1)

            def rows_batch(b):
                pe.wait_ge(S("h0"), TB * b + TB)
                pe.wait_ge(S("keys_known"), b + 1)
                for j in range(TB):
                    last = pe.transpose(pl[:, 0, j * P:(j + 1) * P], h[:, j, :], ident)
                last.then_inc(S("h0_t_ps"), 1)

            def starts(b):
                pe.wait_ge(S("cnt_ready"), b + 1)
                after(pe, "h0_t", b)
                mm(starts_ps, before[:, :], cnt_b[:, :]).then_inc(S("starts_ps"), 1)

            def lists(b, par):
                pe.wait_ge(S("own_ready"), TB * b + TB)
                pe.wait_ge(S("split_ready"), b + 1)
                for j in range(TB):
                    for q in range(CHUNKS):
                        for half_ in range(2):
                            last = mm(lists_ps[:, j, q, :], own[:, TB * par + j, q * P:(q + 1) * P], split_b[:, j, half_, :],
                                      start=half_ == 0, stop=half_ == 1)
                last.then_inc(S("listed_ps"), 1)

            def transpose_keys(b, j, t):
                pe.wait_ge(S(f"g_in{j}"), 16 * CHUNKS * (b + 1))
                after(pe, "out_read", t - 1)
                for q in range(CHUNKS):
                    last = pe.transpose(pt[:, q * P:(q + 1) * P], g[:, j, q, 0:P], ident)
                last.then_inc(S("g_t_ps"), 1)

            def mask(j):
                for lo, hi in parts:
                    mm(ps[:, lo:hi], ones3[0:1, :], big_row[0:1, lo:hi], stop=False)
                    mm(ps[:, lo:hi], big_ident[:, :], own[:, j, lo:hi], start=False, stop=False)

            def mask_by_ends(j):
                for lo, hi in parts:
                    mm(ps[:, lo:hi], ones3[0:2, :], big_row[0:2, lo:hi], stop=False)
                    for marks in (j, TB + j):
                        mm(ps[:, lo:hi], big_ident[:, :], own[:, marks, lo:hi], start=False, stop=False)

            def scores0(t, k):
                pe.wait_ge(S("g_t"), t + 1)
                after(pe, "score", t)
                mask(k)
                for lo, hi in parts:
                    last = mm(ps[:, lo:hi], h_t[:, k // TB, k % TB, :], g_t[:, lo:hi], start=False)
                last.then_inc(S("scores"), 1)

            def transpose_probs(n):
                pe.wait_ge(S("prob"), n + 1)
                for q in range(CHUNKS):
                    last = pe.transpose(pt[:, q * P:(q + 1) * P], prob[:, q * P:(q + 1) * P], ident)
                last.then_inc(S("prob_t_ps"), 1)

            def mix(n, k, out_ps):
                pe.wait_ge(S("prob_t"), n + 1)
                after(pe, "out_read", n)
                for q in range(CHUNKS):
                    last = mm(out_ps, prob_t[:, q * P:(q + 1) * P], g[:, k % TB, q, 0:P],
                              start=q == 0, stop=q == CHUNKS - 1)
                last.then_inc(S("mixed_ps"), 1)

            def rows_tile(t):
                pe.wait_ge(S("h1"), t + 1)
                after(pe, "g_out", t)
                pe.transpose(h1t_ps, h1[:, :], ident).then_inc(S("h1_t_ps"), 1)

            def project(t):
                pe.wait_ge(S("h1_t"), t + 1)
                mm(g_ps, h1_t[:, :], wext[:, :]).then_inc(S("g_ps"), 1)

            pe.wait_ge(S("const_in"), 16)
            pe.wait_ge(S("w_in"), 16)
            pe.wait_ge(S("pe_consts"), 3)
            pe.transpose(pt[:, 0:P], wext[:, 0:P], ident).then_inc(S("w_t_ps"), 1)
            pe.wait_ge(S("a_in"), 16)
            pe.wait_ge(S("w_t"), 1)
            mm(ps[:, 0:2], w_t[:, :], a_col[:, :]).then_inc(S("wa_ps"), 1)
            pe.wait_ge(S("dve_consts"), BITS + 4)
            pe.wait_ge(S("wa"), 1)

            def step(b, j, par):
                t = TB * b + j
                reads, lists_it = holds(b, 0, NB), holds(b - 1, 0, NB)
                if holds(t - 11):
                    mix(t - 11, j - 11, out_ps)
                if lists_it and j == 3:
                    rows_batch(b - 1)
                if lists_it and j == 1:
                    if isinstance(b, int) and b == 1:
                        pe.wait_ge(S("key_red"), KEY_PARTS)
                        mm(mean_ps, mean_w[:, :], key_red[:, :]).then_inc(S("mean0_ps"), 1)
                        pe.wait_ge(S("mean0"), 1)
                    starts(b - 1)
                if holds(t - 14):
                    project(t - 14)
                if reads:
                    pack(b, j, 0)
                    pack(b, j, 1)
                if holds(t - 9):
                    transpose_keys(b + (j - 9) // TB, (j - 9) % TB, t - 9)
                if reads:
                    pack(b, j, 2)
                if holds(t - 13):
                    rows_tile(t - 13)
                if holds(t - 10):
                    pe.wait_ge(S("g_t"), min(t - 8, NT) if isinstance(t, int) else t - 8)
                    if isinstance(t, int) and t - 9 == NT:
                        pe.wait_ge(S("out_read"), NT - 1)
                    transpose_probs(t - 10)
                if lists_it and j == 2:
                    lists(b - 1, 1 - par)
                if reads:
                    pack(b, j, 3)
                if holds(t - 9):
                    if j == 1:
                        pe.wait_ge(S("h0_t"), b - 1)
                    scores0(t - 9, (TB * par + j - 9) % (2 * TB))
            read_and_attend(pe, step)
            pe.wait_ge(S("bad_ready"), 1)
            mm(flag_ps, bad[:, 0:1], mean_w[:, 0:1]).then_inc(S("flag_ps"), 1)
            pe.wait_ge(S("key_sum"), NT)
            pe.wait_ge(S("flag_ready"), 1)
            dense = pe.value_load(flag[0:1, 0:1], min_val=0, max_val=1)
            with pe.If(dense == 0):
                mm(mean_ps, mean_w[:, :], key_sum[:, :]).then_inc(S("mean1_ps"), 1)
                pe.wait_ge(S("mean1"), 1)

                def scores1(b, j):
                    t = TB * b + j
                    n = NT + t
                    pe.wait_ge(S("marked"), t + 1)
                    after(pe, "score", n)
                    mask_by_ends(j)
                    pe.wait_ge(S(f"g_in{j}"), 16 * CHUNKS * (NB + b + 1))
                    for q in range(CHUNKS):
                        last = mm(ps[:, q * P:(q + 1) * P], g[:, j, q, P:P + 1].to_broadcast([P, P]), ident,
                                  start=False, stop=(q + 1) * P in (512, EDGES))
                    last.then_inc(S("scores"), 1)

                def step1(b, j):
                    t = TB * b + j
                    if holds(t - 2):
                        mix(NT + t - 2, j - 2, out1_ps)
                    if holds(t):
                        scores1(b, j)
                    if holds(t - 1):
                        transpose_probs(NT + t - 1)
                attend(pe, step1)
            with pe.If(dense != 0):
                dense_pe(pe)

        @block.vector
        def _(dve):
            TS, STT, TT = dve.tensor_scalar, dve.scalar_tensor_tensor, dve.tensor_tensor

            def top8(i, j, bank):
                dve.wait_ge(S("packed"), 2 * i + bank + 1)
                settled(dve)
                for q in range(2):
                    o = 8 * (2 * bank + q)
                    last = dve.max(cand[:, j, 0, o:o + 8], pk[:, bank, q * QW:(q + 1) * QW])
                last.then_inc(S("maxed"), 1)

            def run_starts(k, t):
                return TS(own[:, k, :], position[:, :], start_all[:, ds(t, 1)], None, ALU.is_ge)

            def rows_batch(b):
                link = linker(dve, "rows_step", b, 1)
                settled(dve)
                for j in range(TB):
                    last = dve.bn_stats(stats[:, j, :], row(xs, TB * b + j))
                link(last)
                settled(dve)
                for j in range(TB):
                    last = dve.bn_aggr(mv[:, j, :], stats[:, j, :])
                last.then_inc(S("var0"), 1)

            def rows_shift(b):
                dve.wait_ge(S("var0"), b + 1)
                dve.wait_ge(S("rstd0"), b + 1)
                STT(nmr[:, :], mv[:, :, 0], -1.0, rstd[:, :], ALU.mult, ALU.mult).then_inc(S("nmr0"), 1)

            def codes(b):
                link = linker(dve, "code_step", b, CODE_LINKS)
                dve.wait_ge(S("maxed"), 2 * TB * (b + 1))
                for lv in range(1, LEVELS):
                    above_v = cand[:, :, lv - 1, :]
                    tb = top_bit[:, lv - 1, :, :]
                    link(TS(tb.bitcast(i32), above_v.bitcast(i32), 0x7F800000, None, ALU.bitwise_and))
                    link(TT(cand[:, :, lv, :], above_v, tb, ALU.subtract))
                TS(cand_i[:, 1, :], cand_int, 23 - IDX_BITS, 255 << IDX_BITS, ALU.logical_shift_right, ALU.bitwise_and)
                link(dve.tensor_copy(cand_i[:, 0, :], cand_v))
                link(TS(cand_i[:, 0, :], cand_i[:, 0, :], (1 << IDX_BITS) - 1, None, ALU.bitwise_and))
                TS(code_f[:, :], cand_v, float(1 << IDX_BITS), None, ALU.is_ge)
                link(STT(cand_i[:, 0, :], cand_i[:, 1, :], float(1 - ((127 + IDX_BITS) << IDX_BITS)), cand_i[:, 0, :],
                         ALU.add, ALU.add))
                TT(code[:, :, :].rearrange("p t c -> p (t c)"), cand_i[:, 0, :], code_f[:, :], ALU.mult)\
                    .then_inc(S("coded"), 1)
                assert link.count[0] == CODE_LINKS, link.count

            def near_rows(b, par):
                link = linker(dve, "near_step", b, NEAR_LINKS)
                dve.wait_ge(S("coded"), b + 1)
                settled(dve)
                for j in range(TB):
                    last = dve.max(near[:, j, 0:8], code[:, j, :])
                link(last)
                settled(dve)
                for j in range(TB):
                    last = dve.match_replace(code2[:, j, :], near[:, j, 0:8], code[:, j, :], 0.0)
                link(last)
                settled(dve)
                for j in range(TB):
                    last = dve.max(near[:, j, 8:16], code2[:, j, :])
                link(last)
                link(TS(is_near[:, :, :], near[:, :, 0:SLOTS], 0.0, None, ALU.is_gt))
                link(dve.tensor_reduce(cnt[:, :], is_near[:, :, :], AX.X, ALU.add))
                dve.tensor_copy(cnt_b[:, :], cnt[:, :]).then_inc(S("cnt_ready"), 1)
                TS(empty_all[:, ds(TB * b, TB)], cnt[:, :], 0.0, None, ALU.is_equal)
                TS(some_all[:, ds(TB * b, TB)], cnt[:, :], 0.0, None, ALU.is_gt)
                dve.wait_ge(S("signs_done"), 4 * TB * (b + 1))
                dve.tensor_reduce(deg[:, 0, :], signs[:, par, :, :], AX.X, ALU.add).then_inc(S("degree_read"), 1)
                dve.wait_ge(S("degree_read"), b + 1)
                link(STT(deg[:, 1, :], cnt[:, :], 2.0, deg[:, 0, :], ALU.mult, ALU.subtract))
                link(TS(deg[:, 2, :], deg[:, 1, :], float(N), 0.0, ALU.subtract, ALU.not_equal))
                assert link.count[0] == NEAR_LINKS, link.count

            def own_runs(b, par):
                link = linker(dve, "own_step", b, OWN_LINKS)
                dve.wait_ge(S("starts_ps"), b + 1)
                dve.tensor_copy(near[:, :, SLOTS], starts_ps)
                dve.tensor_copy(start_all[:, ds(TB * b, TB)], starts_ps)
                link(TT(end_all[:, ds(TB * b, TB)], starts_ps, cnt[:, :], ALU.add))
                link(STT(deg[:, 3, :], end_all[:, ds(TB * b, TB)], float(EDGES), deg[:, 2, :], ALU.is_gt, ALU.add))
                link(dve.tensor_reduce(bad_n[:, 0:1], deg[:, 3, :], AX.X, ALU.add))
                link(TT(bad[:, :], bad[:, :], bad_n[:, 0:1], ALU.add))
                link(dve.tensor_copy(near_i[:, :, :], near[:, :, :]))
                TS(split_i[:, :, 0, :], near_i[:, :, :], 0x3FC0, None, ALU.bitwise_and)
                link(TS(split_i[:, :, 1, :], near_i[:, :, :], 63, None, ALU.bitwise_and))
                dve.tensor_copy(split_b[:, :, :, :], split_i[:, :, :, :]).then_inc(S("split_ready"), 1)
                after(dve, "scores", TB * (b - 1))
                for j in range(TB):
                    run_starts(TB * par + j, TB * b + j)
                    TS(until_end[:, j, :], position[:, :], end_all[:, ds(TB * b + j, 1)], None, ALU.is_lt)\
                        .then_inc(S("run_ends"), 1)
                assert link.count[0] == OWN_LINKS, link.count

            def rows_turned(b, par):
                dve.wait_ge(S("h0_t_ps"), b + 1)
                dve.tensor_copy(h_t[:, par, :, :].rearrange("p t d -> p (t d)"), pl[:, 0, :]).then_inc(S("h0_t"), 1)

            def edge_keys(b):
                link = linker(dve, "key_step", b, KEY_LINKS)
                dve.wait_ge(S("listed_ps"), b + 1)
                edge_b = c("edge").rearrange("p (t c) -> p t c", t=1).to_broadcast([P, TB, CHUNKS])
                link(TT(my_slot[:, :, :], edge_b, lists_ps[:, :, :, SLOTS], ALU.subtract))
                v3 = "p t c s -> p (t c) s"
                for j in range(TB):
                    last = TT(pick[:, j, :, :], c("slot").rearrange("p (c s) -> p c s", c=CHUNKS),
                              my_slot[:, j, :].rearrange("p (c o) -> p c o", o=1).to_broadcast([P, CHUNKS, SLOTS]), ALU.is_equal)
                link(last)
                link(TT(pick[:, :, :, :].rearrange(v3), pick[:, :, :, :].rearrange(v3),
                        lists_ps[:, :, :, 0:SLOTS].rearrange(v3), ALU.mult))
                link(dve.tensor_reduce(key_f[:, :, :].rearrange("p t c -> p (t c)"), pick[:, :, :, :].rearrange(v3), AX.X, ALU.add))
                TS(key_idx[:, ds(TB * CHUNKS * b, TB * CHUNKS)], key_f[:, :, :].rearrange("p t c -> p (t c)"), -1.0, 0.0,
                   ALU.add, ALU.max).then_inc(S("keys_known"), 1)
                assert link.count[0] == KEY_LINKS, link.count

            def keys_transposed(t):
                dve.wait_ge(S("g_t_ps"), t + 1)
                after(dve, "scores", t)
                dve.tensor_copy(g_t[:, :], pt[:, 0:EDGES]).then_inc(S("g_t"), 1)

            def inverse_begin(n, k):
                dve.wait_ge(S("prob"), n + 1)
                dve.reciprocal(inv[:, k % 2:k % 2 + 1], prob_sum[:, k % 2:k % 2 + 1]).then_inc(S("inverse"), 1)

            def inverse_end(n, t, k):
                dve.wait_ge(S("inverse"), n + 1)
                TT(inv_some[:, k % 2:k % 2 + 1], inv[:, k % 2:k % 2 + 1], some_all[:, ds(t, 1)], ALU.mult)\
                    .then_inc(S("inverse_some"), 1)

            def maximum(n, k):
                dve.wait_ge(S("score"), n + 1)
                after(dve, "prob", n - 1)
                dve.tensor_reduce(neg_max[:, k % 2:k % 2 + 1], score[:, :], AX.X, ALU.max, negate=True)\
                    .then_inc(S("maximum"), 1)

            def soft(n, k):
                dve.wait_ge(S("maximum"), n + 1)
                STT(bias[:, k % 2:k % 2 + 1], neg_max[:, k % 2:k % 2 + 1], LEAK, neg_max[:, k % 2:k % 2 + 1],
                    ALU.mult, ALU.min)
                after(dve, "prob", n)
                STT(leaky[:, :], score[:, :], LEAK, score[:, :], ALU.mult, ALU.max).then_inc(S("leaky"), 1)

            def probs_transposed(n):
                dve.wait_ge(S("prob_t_ps"), n + 1)
                after(dve, "mixed_ps", n)
                dve.tensor_copy(prob_t[:, :], pt[:, 0:EDGES]).then_inc(S("prob_t"), 1)

            def output_begin(t, k):
                dve.wait_ge(S("inverse_some"), t + 1)
                dve.wait_ge(S("mixed_ps"), t + 1)
                STT(mixed[:, k % 2, :], out_ps, inv_some[:, k % 2:k % 2 + 1], row(xs, t), ALU.mult, ALU.add)\
                    .then_inc(S("out_read"), 1)

            def output_end(t, k):
                dve.wait_ge(S("out_read"), t + 1)
                STT(row(xs, t), mean0[:, :], empty_all[:, ds(t, 1)], mixed[:, k % 2, :], ALU.mult, ALU.add)\
                    .then_inc(S("output0"), 1)

            def row_stats(t):
                dve.wait_ge(S("output0"), t + 1)
                settled(dve)
                dve.bn_stats(stats1[:, :], row(xs, t)).then_inc(S("row_stats"), 1)

            def row_mean(t):
                dve.wait_ge(S("row_stats"), t + 1)
                after(dve, "h1", t)
                settled(dve)
                dve.bn_aggr(mv1[:, :], stats1[:, :]).then_inc(S("row_mean"), 1)

            def row_nmean(t):
                dve.wait_ge(S("row_mean"), t + 1)
                TS(nmean1[:, :], mv1[:, 0:1], -1.0, None, ALU.mult).then_inc(S("var1"), 1)

            def rows_transposed(t):
                dve.wait_ge(S("h1_t_ps"), t + 1)
                after(dve, "g_ps", t)
                dve.tensor_copy(h1_t[:, :], h1t_ps).then_inc(S("h1_t"), 1)

            def keys1(t, b, j):
                dve.wait_ge(S("g_ps"), t + 1)
                if holds(t - 2):
                    dve.wait_ge(S(f"g_stored{j % 2}"), 16 * pair(b, j))
                    dve.wait_ge(S("key_sum"), t - 1)
                dve.tensor_copy(s_all[:, ds(t, 1)], g_ps[:, GW:GW + 1])
                dve.tensor_copy(g_out[:, j % 2, :], g_ps[:, 0:GW]).then_inc(S("g_out"), 1)

            dve.memset(key_sum[:, :], 0.0).then_inc(S("zeroed"), 1)
            dve.memset(bad[:, :], 0.0).then_inc(S("zeroed"), 1)
            dve.memset(key_red[:, :], 0.0).then_inc(S("zeroed"), 1)
            dve.wait_ge(S("const_in"), 16)
            dve.wait_ge(S("raw_const_in"), 32)
            for k in range(BITS):
                TS(pack_w[:, k, :], ident, float(1 << (k + IDX_BITS - 1)), None, ALU.mult).then_inc(S("dve_consts"), 1)
            TS(big_ident[:, :], ident, BIG, None, ALU.mult).then_inc(S("dve_consts"), 1)
            dve.tensor_copy(before[:, :], c("before")).then_inc(S("dve_consts"), 1)
            dve.tensor_copy(pack_c[:, :], c("packed")[0:3, :]).then_inc(S("dve_consts"), 1)
            dve.tensor_copy(position[:, :], c("position")).then_inc(S("dve_consts"), 1)
            dve.wait_ge(S("w_t_ps"), 1)
            dve.tensor_copy(w_t[:, :], pt[:, 0:P]).then_inc(S("w_t"), 1)
            dve.wait_ge(S("wa_ps"), 1)
            dve.tensor_copy(wext[:, P:P + 1], ps[:, 1:2])
            dve.tensor_copy(wext[:, P + 1:P + 2], ps[:, 0:1]).then_inc(S("wa"), 1)
            dve.wait_ge(S("dve_consts"), BITS + 4)
            dve.wait_ge(S("zeroed"), 3)
            for k in range(KEY_PARTS):
                dve.wait_ge(S(f"keys_in{k}"), 16)
                after(dve, "key_red", k)
                dve.tensor_reduce(key_part[:, :], all_keys[:, k * KEY_TILES:(k + 1) * KEY_TILES, :].rearrange("p t d -> p d t"),
                                  AX.X, ALU.add).then_inc(S("key_part"), 1)
                dve.wait_ge(S("key_part"), k + 1)
                TT(key_red[:, :], key_red[:, :], key_part[:, :], ALU.add).then_inc(S("key_red"), 1)

            def step(b, j, par):
                t = TB * b + j
                lists_it = holds(b - 1, 0, NB)
                if holds(t - 10):
                    soft(t - 10, j - 10)
                if holds(t - 14):
                    keys1(t - 14, b, j - 14)
                if lists_it and j == 1:
                    rows_shift(b - 1)
                if holds(t - 9):
                    keys_transposed(t - 9)
                if holds(t - 12):
                    row_mean(t - 12)
                if lists_it and j == 0:
                    if isinstance(b, int) and b == 1:
                        dve.wait_ge(S("x_in"), 16)
                    rows_batch(b - 1)
                if holds(t - 12):
                    row_nmean(t - 12)
                if holds(t - 13):
                    rows_transposed(t - 13)
                if lists_it and j == 1:
                    own_runs(b - 1, 1 - par)
                if lists_it and j == 3:
                    rows_turned(b - 1, 1 - par)
                if holds(t - 10):
                    inverse_begin(t - 10, j - 10)
                if holds(t - 11):
                    output_end(t - 11, j - 11)
                if holds(t - 10):
                    probs_transposed(t - 10)
                if lists_it and j == 2:
                    edge_keys(b - 1)
                if lists_it and j == 0:
                    near_rows(b - 1, 1 - par)
                if holds(t - 11):
                    row_stats(t - 11)
                if holds(b, 0, NB):
                    for bank in range(2):
                        top8(t, j, bank)
                if holds(b, 0, NB) and j == 3:
                    codes(b)
                if holds(t - 10):
                    inverse_end(t - 10, t - 10, j - 10)
                if holds(t - 9):
                    maximum(t - 9, j - 9)
                if holds(t - 10):
                    output_begin(t - 10, j - 10)
                if isinstance(b, int) and b == 1 and j == 0:
                    dve.wait_ge(S("mean0_ps"), 1)
                    dve.tensor_copy(mean0[:, :], mean_ps).then_inc(S("mean0"), 1)
                    dve.wait_ge(S("mean0"), 1)
            read_and_attend(dve, step)
            dve.wait_ge(S("own_step"), NB * OWN_LINKS)
            dve.memset(bad_n[:, 1:2], 1.0).then_inc(S("bad_ready"), 1)
            dve.wait_ge(S("flag_ps"), 1)
            TS(flag[:, :], flag_ps, 0.0, None, ALU.is_gt).then_inc(S("flag_ready"), 1)
            dve.wait_ge(S("flag_ready"), 1)
            dense = dve.value_load(flag[0:1, 0:1], min_val=0, max_val=1)
            with dve.If(dense == 0):
                dve.wait_ge(S("mean1_ps"), 1)
                dve.tensor_copy(mean1[:, :], mean_ps).then_inc(S("mean1"), 1)

                def mark(t, j):
                    after(dve, "scores", NT + t - TB + 1)
                    run_starts(j, t)
                    TS(own[:, TB + j, :], position[:, :], end_all[:, ds(t, 1)], None, ALU.is_lt).then_inc(S("marked"), 1)

                def output1_begin(t, k):
                    dve.wait_ge(S("inverse_some"), NT + t + 1)
                    dve.wait_ge(S("mixed_ps"), NT + t + 1)
                    TS(above[:, k % 2, :], out1_ps, inv_some[:, k % 2:k % 2 + 1], None, ALU.mult).then_inc(S("out_read"), 1)

                def output1_end(t, k):
                    link = linker(dve, "output1_step", t, 1)
                    dve.wait_ge(S("out_read"), NT + t + 1)
                    link(STT(mixed[:, k % 2, :], mean1[:, :], empty_all[:, ds(t, 1)], above[:, k % 2, :], ALU.mult, ALU.add))
                    TS(below[:, k % 2, :], mixed[:, k % 2, :], 0.0, None, ALU.min).then_inc(S("below"), 1)
                    STT(above[:, k % 2, :], mixed[:, k % 2, :], 0.0, row(xs, t), ALU.max, ALU.add).then_inc(S("above"), 1)

                def elu(t, b, j):
                    dve.wait_ge(S("grown"), t + 1)
                    dve.wait_ge(S("above"), t + 1)
                    if holds(t - 2):
                        dve.wait_ge(S(f"out_stored{j % 2}"), 16 * pair(b, j))
                    STT(y[:, j % 2, :], grown[:, j % 2, :], -1.0, above[:, j % 2, :], ALU.add, ALU.add).then_inc(S("y_ready"), 1)

                def step1(b, j):
                    t = TB * b + j
                    if holds(t):
                        mark(t, j)
                    if holds(t - 2):
                        inverse_begin(NT + t - 2, j - 2)
                    if holds(t - 3):
                        elu(t - 3, b, j - 3)
                    if holds(t - 2):
                        inverse_end(NT + t - 2, t - 2, j - 2)
                        output1_begin(t - 2, j - 2)
                        output1_end(t - 2, j - 2)
                    if holds(t):
                        maximum(NT + t, j)
                        soft(NT + t, j)
                attend(dve, step1)
            with dve.If(dense != 0):
                dense_dve(dve)


def kernel(x, adj, L0_gnn_ks, L1_gnn_W, L1_gnn_a):
    import numpy as np
    import concourse.bacc as bacc
    from concourse.bass_utils import run_bass_kernel_spmd

    nc = bacc.Bacc("TRN2", target_bir_lowering=False, num_devices=1)
    arrays = {"x": x, "adj": adj, "ks": L0_gnn_ks, "w": L1_gnn_W, "a": L1_gnn_a, "table": constant_table(x.shape[0])}
    arrays = {name: np.ascontiguousarray(v) for name, v in arrays.items()}
    args = [nc.dram_tensor(name, v.shape, mybir.dt.from_np(v.dtype), kind="ExternalInput").ap()
            for name, v in arrays.items()]
    out = nc.dram_tensor("out", x.shape, mybir.dt.float32, kind="ExternalOutput").ap()
    build(nc, *args, out)
    return run_bass_kernel_spmd(nc, [arrays], core_ids=[0]).results[0]["out"]
```
